# Optimizing a Trainium2 kernel written in Bass

```python
import numpy as np
import jax
import jax.numpy as jnp

def _softmax(x, axis=-1):
    return jax.nn.softmax(x, axis=axis)

def _gelu(x):
    return jax.nn.gelu(x, approximate=True)

def _silu(x):
    return jax.nn.silu(x)

def _sigmoid(x):
    return jax.nn.sigmoid(x)

def _layernorm(x, axis=-1, eps=1e-05):
    m = jnp.mean(x, axis=axis, keepdims=True)
    v = jnp.var(x, axis=axis, keepdims=True)
    return (x - m) / jnp.sqrt(v + eps)

def _scatter_add(tgt, idx, src, axis=0):
    return tgt.at[idx].add(src)

def _segment_sum(src, seg, n):
    return jax.ops.segment_sum(src, seg, n)
kernel_name = 'mk_gnn_resnorm_d2_gnn_r64_0b9cb9'

def setup_inputs(seed: int=0):
    np.random.seed(seed)
    _w = jnp.asarray

    def _rec_inputs():
        import jax
        import jax.numpy as jnp
        _gk = jax.random.key(seed)
        x = -0.0009044 + 1 * jax.random.normal(jax.random.fold_in(_gk, 1), (100000, 160), jnp.float32)
        src = jax.random.randint(jax.random.fold_in(_gk, 2), (25000,), 0, 100000, jnp.int32)
        dst = jax.random.randint(jax.random.fold_in(_gk, 3), (25000,), 0, 100000, jnp.int32)
        _o = jnp.argsort(dst, stable=True)
        src = src[_o]
        dst = dst[_o]
        edge_attr_4 = -0.000149047 + 1.00006 * jax.random.normal(jax.random.fold_in(_gk, 12), (25000, 4), jnp.float32)
        edge_attr_64 = 0.000127647 + 1.00004 * jax.random.normal(jax.random.fold_in(_gk, 13), (25000, 64), jnp.float32)
        edge_attr_8 = 0.000735704 + 1.0001 * jax.random.normal(jax.random.fold_in(_gk, 14), (25000, 8), jnp.float32)
        node_vec1 = jax.random.uniform(jax.random.fold_in(_gk, 15), (100000, 1), jnp.float32, 0.0, 1)
        return (x, src, dst, edge_attr_4, edge_attr_64, edge_attr_8, node_vec1)
    x, src, dst, edge_attr_4, edge_attr_64, edge_attr_8, node_vec1 = _rec_inputs()

    def _L0_gnn_setup():
        import jax, jax.numpy as jnp
        import numpy as np
        N_NODES = 10000
        N_EDGES = 5000
        NUM_NEIGHBORS = 32.0
        INV_SQRT3 = 1.0 / np.sqrt(3.0)

        def _fctp_scalar_attr(xs, xv, Ws, Wv, a):
            out_s = xs @ Ws * (a / np.sqrt(xs.shape[1]))[:, None]
            out_v = jnp.einsum('nuc,uw->nwc', xv, Wv) * (a / np.sqrt(xv.shape[1]))[:, None, None]
            return (out_s, out_v)
        key = jax.random.key(seed)
        ks = jax.random.split(key, 16)
        f32 = jnp.float32
        return {'node_input': jax.random.normal(ks[0], (N_NODES, 160), f32), 'node_attr': jnp.ones((N_NODES, 1), f32), 'edge_attr': jax.random.normal(ks[1], (N_EDGES, 4), f32), 'edge_scalar_attr': jax.random.normal(ks[2], (N_EDGES, 8), f32), 'Wsc0': jax.random.normal(ks[3], (64, 64), f32), 'Wsc1': jax.random.normal(ks[4], (32, 32), f32), 'Wl1_0': jax.random.normal(ks[5], (64, 64), f32), 'Wl1_1': jax.random.normal(ks[6], (32, 32), f32), 'Wfc1': jax.random.normal(ks[7], (8, 64), f32), 'Wfc2': jax.random.normal(ks[8], (64, 64), f32), 'Wfc3': jax.random.normal(ks[9], (64, 192), f32), 'Wl2_s': jax.random.normal(ks[10], (96, 64), f32), 'Wl2_v': jax.random.normal(ks[11], (96, 32), f32), 'Wa': jax.random.normal(ks[12], (96, 1), f32), 'edge_src': jax.random.randint(ks[13], (N_EDGES,), 0, N_NODES), 'edge_dst': jax.random.randint(ks[14], (N_EDGES,), 0, N_NODES)}
    _L0_gnn_all = _L0_gnn_setup()
    _L0_gnn_in = {k: v for k, v in _L0_gnn_all.items() if k in ('Wsc0', 'Wsc1', 'Wl1_0', 'Wl1_1', 'Wfc1', 'Wfc2', 'Wfc3', 'Wl2_s', 'Wl2_v', 'Wa')}
    del _L0_gnn_all

    def _L1_gnn_setup():
        import jax, jax.numpy as jnp
        import numpy as np
        N, E = (625, 10000)
        S_IN, V_IN = (64, 32)
        S_MID, V_MID = (96, 128)
        S_OUT, V_OUT = (96, 32)
        R = 64
        FC_HID = 64
        W_NUMEL = 64 + 64 + 32 + 32 + 32
        NUM_NEIGHBORS = 16.0

        def _inv(d):
            return 1.0 / jnp.sqrt(jnp.float32(d))

        def _forward(node_features, node_attr, edge_attr, edge_scalars, lin1_ws, lin1_wv, fc_w1, fc_w2, sc_ws, sc_wv, lin2_ws, lin2_wv, edge_src, edge_dst):
            n = node_features.shape[0]
            s = node_features[:, :S_IN]
            v = node_features[:, S_IN:].reshape(n, V_IN, 3)
            a = node_attr
            sc_s = s @ sc_ws * a * _inv(S_IN)
            sc_v = jnp.einsum('nci,cd->ndi', v, sc_wv) * a[:, :, None] * _inv(V_IN)
            h_s = s @ lin1_ws * a * _inv(S_IN)
            h_v = jnp.einsum('nci,cd->ndi', v, lin1_wv) * a[:, :, None] * _inv(V_IN)
            hid = jax.nn.silu(edge_scalars @ fc_w1 * _inv(R))
            w = hid @ fc_w2 * _inv(FC_HID)
            w1, w2, w3, w4, w5 = jnp.split(w, [64, 128, 160, 192], axis=-1)
            es = h_s[edge_src]
            ev = h_v[edge_src]
            e0 = edge_attr[:, :1]
            e1 = edge_attr[:, 1:4]
            m_s1 = w1 * es * e0
            m_s2 = w4 * jnp.einsum('eci,ei->ec', ev, e1) * _inv(3)
            m_v1 = (w2 * es)[:, :, None] * e1[:, None, :]
            m_v2 = w3[:, :, None] * ev * e0[:, :, None]
            m_v3 = w5[:, :, None] * jnp.cross(ev, e1[:, None, :]) * _inv(2)
            mid_s = jnp.concatenate([m_s1, m_s2], axis=-1)
            mid_v = jnp.concatenate([m_v1, m_v2, m_v3], axis=1)
            inv_nn = 1.0 / jnp.sqrt(jnp.float32(NUM_NEIGHBORS))
            agg_s = jax.ops.segment_sum(mid_s, edge_dst, num_segments=n) * inv_nn
            agg_v = jax.ops.segment_sum(mid_v, edge_dst, num_segments=n) * inv_nn
            o_s = agg_s @ lin2_ws * a * _inv(S_MID)
            o_v = jnp.einsum('nci,cd->ndi', agg_v, lin2_wv) * a[:, :, None] * _inv(V_MID)
            pre_s = sc_s + o_s
            pre_v = sc_v + o_v
            scalars = jax.nn.silu(pre_s[:, :64])
            gates = jax.nn.sigmoid(pre_s[:, 64:96])
            gated = gates[:, :, None] * pre_v
            return jnp.concatenate([scalars, gated.reshape(n, 3 * V_OUT)], axis=-1)
        key = jax.random.key(seed)
        ks = jax.random.split(key, 13)
        return {'node_features': jax.random.normal(ks[0], (N, S_IN + 3 * V_IN), jnp.float32), 'node_attr': jnp.ones((N, 1), jnp.float32), 'edge_src': jax.random.randint(ks[1], (E,), 0, N), 'edge_dst': jax.random.randint(ks[2], (E,), 0, N), 'edge_attr': jax.random.normal(ks[3], (E, 4), jnp.float32), 'edge_scalars': jax.random.normal(ks[4], (E, R), jnp.float32), 'lin1_ws': jax.random.normal(ks[5], (S_IN, S_IN), jnp.float32), 'lin1_wv': jax.random.normal(ks[6], (V_IN, V_IN), jnp.float32), 'fc_w1': jax.random.normal(ks[7], (R, FC_HID), jnp.float32), 'fc_w2': jax.random.normal(ks[8], (FC_HID, W_NUMEL), jnp.float32), 'sc_ws': jax.random.normal(ks[9], (S_IN, S_OUT), jnp.float32), 'sc_wv': jax.random.normal(ks[10], (V_IN, V_OUT), jnp.float32), 'lin2_ws': jax.random.normal(ks[11], (S_MID, S_OUT), jnp.float32), 'lin2_wv': jax.random.normal(ks[12], (V_MID, V_OUT), jnp.float32)}
    _L1_gnn_all = _L1_gnn_setup()
    _L1_gnn_in = {k: v for k, v in _L1_gnn_all.items() if k in ('lin1_ws', 'lin1_wv', 'fc_w1', 'fc_w2', 'sc_ws', 'sc_wv', 'lin2_ws', 'lin2_wv')}
    del _L1_gnn_all
    return {'x': x, 'src': src, 'dst': dst, 'edge_attr_4': edge_attr_4, 'edge_attr_64': edge_attr_64, 'edge_attr_8': edge_attr_8, 'node_vec1': node_vec1, 'L0_gnn_Wsc0': _L0_gnn_in['Wsc0'], 'L0_gnn_Wsc1': _L0_gnn_in['Wsc1'], 'L0_gnn_Wl1_0': _L0_gnn_in['Wl1_0'], 'L0_gnn_Wl1_1': _L0_gnn_in['Wl1_1'], 'L0_gnn_Wfc1': _L0_gnn_in['Wfc1'], 'L0_gnn_Wfc2': _L0_gnn_in['Wfc2'], 'L0_gnn_Wfc3': _L0_gnn_in['Wfc3'], 'L0_gnn_Wl2_s': _L0_gnn_in['Wl2_s'], 'L0_gnn_Wl2_v': _L0_gnn_in['Wl2_v'], 'L0_gnn_Wa': _L0_gnn_in['Wa'], 'L1_gnn_lin1_ws': _L1_gnn_in['lin1_ws'], 'L1_gnn_lin1_wv': _L1_gnn_in['lin1_wv'], 'L1_gnn_fc_w1': _L1_gnn_in['fc_w1'], 'L1_gnn_fc_w2': _L1_gnn_in['fc_w2'], 'L1_gnn_sc_ws': _L1_gnn_in['sc_ws'], 'L1_gnn_sc_wv': _L1_gnn_in['sc_wv'], 'L1_gnn_lin2_ws': _L1_gnn_in['lin2_ws'], 'L1_gnn_lin2_wv': _L1_gnn_in['lin2_wv']}

def reference(x, src, dst, edge_attr_4, edge_attr_64, edge_attr_8, node_vec1, L0_gnn_Wsc0, L0_gnn_Wsc1, L0_gnn_Wl1_0, L0_gnn_Wl1_1, L0_gnn_Wfc1, L0_gnn_Wfc2, L0_gnn_Wfc3, L0_gnn_Wl2_s, L0_gnn_Wl2_v, L0_gnn_Wa, L1_gnn_lin1_ws, L1_gnn_lin1_wv, L1_gnn_fc_w1, L1_gnn_fc_w2, L1_gnn_sc_ws, L1_gnn_sc_wv, L1_gnn_lin2_ws, L1_gnn_lin2_wv):
    import jax
    import jax.numpy as jnp

    def _L0_gnn_ref(node_input, node_attr, edge_attr, edge_scalar_attr, Wsc0, Wsc1, Wl1_0, Wl1_1, Wfc1, Wfc2, Wfc3, Wl2_s, Wl2_v, Wa, edge_src, edge_dst):
        import jax, jax.numpy as jnp
        import numpy as np
        N_NODES = 10000
        N_EDGES = 5000
        NUM_NEIGHBORS = 32.0
        INV_SQRT3 = 1.0 / np.sqrt(3.0)

        def _fctp_scalar_attr(xs, xv, Ws, Wv, a):
            out_s = xs @ Ws * (a / np.sqrt(xs.shape[1]))[:, None]
            out_v = jnp.einsum('nuc,uw->nwc', xv, Wv) * (a / np.sqrt(xv.shape[1]))[:, None, None]
            return (out_s, out_v)
        N = node_input.shape[0]
        a = node_attr[:, 0]
        xs = node_input[:, :64]
        xv = node_input[:, 64:].reshape(N, 32, 3)
        sc_s, sc_v = _fctp_scalar_attr(xs, xv, Wsc0, Wsc1, a)
        f_s, f_v = _fctp_scalar_attr(xs, xv, Wl1_0, Wl1_1, a)
        h = jax.nn.gelu(edge_scalar_attr @ Wfc1 / np.sqrt(8.0))
        h = jax.nn.gelu(h @ Wfc2 / np.sqrt(64.0))
        w = h @ Wfc3 / np.sqrt(64.0)
        w0, w1, w2, w3 = (w[:, :64], w[:, 64:128], w[:, 128:160], w[:, 160:192])
        gs = f_s[edge_src]
        gv = f_v[edge_src]
        y0 = edge_attr[:, 0]
        y1 = edge_attr[:, 1:4]
        mid0 = w0 * gs * y0[:, None]
        mid1 = w3 * jnp.einsum('euc,ec->eu', gv, y1) * INV_SQRT3
        mid2 = (w1 * gs)[:, :, None] * y1[:, None, :]
        mid3 = w2[:, :, None] * gv * y0[:, None, None]
        inv = 1.0 / np.sqrt(NUM_NEIGHBORS)
        seg = lambda x: jax.ops.segment_sum(x, edge_dst, num_segments=N) * inv
        ns0, ns1, nv2, nv3 = (seg(mid0), seg(mid1), seg(mid2), seg(mid3))
        mid_s = jnp.concatenate([ns0, ns1], axis=1)
        mid_v = jnp.concatenate([nv2, nv3], axis=1)
        out_s = mid_s @ Wl2_s * (a / np.sqrt(96.0))[:, None]
        out_v = jnp.einsum('nuc,uw->nwc', mid_v, Wl2_v) * (a / np.sqrt(96.0))[:, None, None]
        alpha = mid_s @ Wa * (a / np.sqrt(96.0))[:, None]
        res_s = sc_s + alpha * out_s
        res_v = sc_v + alpha[:, :, None] * out_v
        return jnp.concatenate([res_s, res_v.reshape(N, 96)], axis=1)

    def _L1_gnn_ref(node_features, node_attr, edge_src, edge_dst, edge_attr, edge_scalars, lin1_ws, lin1_wv, fc_w1, fc_w2, sc_ws, sc_wv, lin2_ws, lin2_wv):
        import jax, jax.numpy as jnp
        import numpy as np
        N, E = (625, 10000)
        S_IN, V_IN = (64, 32)
        S_MID, V_MID = (96, 128)
        S_OUT, V_OUT = (96, 32)
        R = 64
        FC_HID = 64
        W_NUMEL = 64 + 64 + 32 + 32 + 32
        NUM_NEIGHBORS = 16.0

        def _inv(d):
            return 1.0 / jnp.sqrt(jnp.float32(d))

        def _forward(node_features, node_attr, edge_attr, edge_scalars, lin1_ws, lin1_wv, fc_w1, fc_w2, sc_ws, sc_wv, lin2_ws, lin2_wv, edge_src, edge_dst):
            n = node_features.shape[0]
            s = node_features[:, :S_IN]
            v = node_features[:, S_IN:].reshape(n, V_IN, 3)
            a = node_attr
            sc_s = s @ sc_ws * a * _inv(S_IN)
            sc_v = jnp.einsum('nci,cd->ndi', v, sc_wv) * a[:, :, None] * _inv(V_IN)
            h_s = s @ lin1_ws * a * _inv(S_IN)
            h_v = jnp.einsum('nci,cd->ndi', v, lin1_wv) * a[:, :, None] * _inv(V_IN)
            hid = jax.nn.silu(edge_scalars @ fc_w1 * _inv(R))
            w = hid @ fc_w2 * _inv(FC_HID)
            w1, w2, w3, w4, w5 = jnp.split(w, [64, 128, 160, 192], axis=-1)
            es = h_s[edge_src]
            ev = h_v[edge_src]
            e0 = edge_attr[:, :1]
            e1 = edge_attr[:, 1:4]
            m_s1 = w1 * es * e0
            m_s2 = w4 * jnp.einsum('eci,ei->ec', ev, e1) * _inv(3)
            m_v1 = (w2 * es)[:, :, None] * e1[:, None, :]
            m_v2 = w3[:, :, None] * ev * e0[:, :, None]
            m_v3 = w5[:, :, None] * jnp.cross(ev, e1[:, None, :]) * _inv(2)
            mid_s = jnp.concatenate([m_s1, m_s2], axis=-1)
            mid_v = jnp.concatenate([m_v1, m_v2, m_v3], axis=1)
            inv_nn = 1.0 / jnp.sqrt(jnp.float32(NUM_NEIGHBORS))
            agg_s = jax.ops.segment_sum(mid_s, edge_dst, num_segments=n) * inv_nn
            agg_v = jax.ops.segment_sum(mid_v, edge_dst, num_segments=n) * inv_nn
            o_s = agg_s @ lin2_ws * a * _inv(S_MID)
            o_v = jnp.einsum('nci,cd->ndi', agg_v, lin2_wv) * a[:, :, None] * _inv(V_MID)
            pre_s = sc_s + o_s
            pre_v = sc_v + o_v
            scalars = jax.nn.silu(pre_s[:, :64])
            gates = jax.nn.sigmoid(pre_s[:, 64:96])
            gated = gates[:, :, None] * pre_v
            return jnp.concatenate([scalars, gated.reshape(n, 3 * V_OUT)], axis=-1)
        return _forward(node_features, node_attr, edge_attr, edge_scalars, lin1_ws, lin1_wv, fc_w1, fc_w2, sc_ws, sc_wv, lin2_ws, lin2_wv, edge_src, edge_dst)
    x = _layernorm(x + _L0_gnn_ref(x, node_vec1, edge_attr_4, edge_attr_8, L0_gnn_Wsc0, L0_gnn_Wsc1, L0_gnn_Wl1_0, L0_gnn_Wl1_1, L0_gnn_Wfc1, L0_gnn_Wfc2, L0_gnn_Wfc3, L0_gnn_Wl2_s, L0_gnn_Wl2_v, L0_gnn_Wa, src, dst), axis=-1)
    x = _layernorm(x + _L1_gnn_ref(x, node_vec1, src, dst, edge_attr_4, edge_attr_64, L1_gnn_lin1_ws, L1_gnn_lin1_wv, L1_gnn_fc_w1, L1_gnn_fc_w2, L1_gnn_sc_ws, L1_gnn_sc_wv, L1_gnn_lin2_ws, L1_gnn_lin2_wv), axis=-1)
    return x

_drawn_inputs = setup_inputs


def setup_inputs(seed=0):
    import zlib

    import numpy as np

    out = dict(_drawn_inputs(seed))
    spreads = {}
    factors = {'edge_attr_4': 4.438,
     'edge_attr_64': 4.761,
     'edge_attr_8': 8.0,
     'L0_gnn_Wl1_0': 8.0,
     'L0_gnn_Wl1_1': 8.0,
     'L0_gnn_Wfc1': 8.0,
     'L0_gnn_Wfc2': 8.0,
     'L0_gnn_Wfc3': 8.0,
     'L0_gnn_Wl2_s': 8.0,
     'L0_gnn_Wl2_v': 8.0,
     'L0_gnn_Wa': 8.0,
     'L1_gnn_lin1_ws': 5.799,
     'L1_gnn_lin1_wv': 6.646,
     'L1_gnn_fc_w1': 4.765,
     'L1_gnn_fc_w2': 4.529,
     'L1_gnn_lin2_ws': 6.574,
     'L1_gnn_lin2_wv': 6.119}
    for name, (base, spread) in spreads.items():
        noise = np.random.default_rng([zlib.crc32(name.encode()), seed]).standard_normal(out[name].shape)
        drawn = base * np.exp(spread * noise) if base else spread * noise
        out[name] = jnp.asarray(drawn.astype(out[name].dtype))
    for name, factor in factors.items():
        out[name] = (out[name] * factor).astype(out[name].dtype)
    return out
```

```python
from contextlib import ExitStack

import concourse.bass as bass
from concourse import mybir

F32 = mybir.dt.float32
BF16 = mybir.dt.bfloat16
I32 = mybir.dt.int32
ALU = mybir.AluOpType
ACT = mybir.ActivationFunctionType
AX = mybir.AxisListType

P = 128
NODES, FEAT = 100000, 160
EDGES = 25000
S, V, C = 64, 32, 3
VC = V * C
TILES = -(-EDGES // P)
TAIL = EDGES - (TILES - 1) * P
PAIRS = TILES // 2
ROWS = 784
TABLE = P * ROWS
SPARE = NODES + 1
ZROWS = 8
NZ = ROWS // ZROWS
AGG0 = FEAT + 1
AGG1 = 96 + VC
MSG0 = AGG0 + V
MSG1 = AGG1 + V
W0N, W1N = 192, 224
J = 4
NGROUPS = -(-NODES // (J * P))
NACT = 2
EPS = 1e-5
assert TILES % 2 == 0 and SPARE + P <= TABLE and NGROUPS % 2 == 0 and ROWS % ZROWS == 0


class Group:

    def __init__(self, g, h, u):
        self.g, self.h, self.u = g, h, u


def passes(engine, count, stages):
    leads = [lead for lead, _ in stages]
    lo, hi = 2 - min(leads), count - 1 - max(leads)
    n = (hi - lo) // 2

    def peeled(p):
        for lead, stage in stages:
            if 0 <= p + lead < count:
                stage(Group(p + lead, (p + lead) % 2, (p + lead) // 2))

    for p in range(-max(leads), lo):
        peeled(p)
    with engine.Fori(0, n) as i:
        for k in range(2):
            for lead, stage in stages:
                c = lo + k + lead
                stage(Group(i * 2 + c, c % 2, i + c // 2))
    for p in range(lo + 2 * n, count - min(leads)):
        peeled(p)


def build(nc, t):
    with ExitStack() as whole:
        k = {}

        def keep(name, shape, dt=F32):
            k[name] = whole.enter_context(nc.sbuf_tensor(name, shape, dt))
            return k[name]

        bank = [whole.enter_context(nc.psum_tensor(f"bank{b}", [P, 512], F32)) for b in range(4)]
        pairs = [whole.enter_context(nc.psum_tensor(f"pair{b}", [P, 2, 512], F32)) for b in range(2)]
        wide, other = pairs
        bank += [other[:, 0, :], other[:, 1, :]]
        keep("ident", [P, P])
        keep("same", [P, TILES, P], BF16)
        keep("src", [P, TILES], I32)
        keep("row", [P, TILES], I32)
        keep("a_src", [P, TILES])
        keep("w0s", [S, 2 * S])
        keep("w0v", [VC, 2 * VC])
        keep("fc1", [8, 64])
        keep("fc2", [64, 64])
        keep("fc3", [64, W0N])
        keep("out0a", [P, MSG0])
        keep("out0b", [P, AGG0])
        keep("w1s", [S, S])
        keep("w1v", [VC, 5 * V])
        keep("gfc1", [64, 64])
        keep("gfc2", [64, W1N])
        keep("out1a", [P, MSG1])
        keep("out1b", [P, AGG1])
        keep("out1c", [VC, VC])
        keep("sc1s", [S, 96])
        keep("sc1v", [VC, VC])
        prepare(nc, t, k, bank, wide)
        edges0(nc, t, k, bank, wide)
        if t.get("stop") == 0:
            return
        edges1(nc, t, k, bank, wide)
        if t.get("stop") == 1:
            return
        nodes(nc, t, k, bank, wide, other)


def phase(nc):
    ctx = ExitStack()
    sb = lambda name, shape, dt=F32: ctx.enter_context(nc.sbuf_tensor(name, shape, dt))
    sem = lambda name: ctx.enter_context(nc.semaphore(name))
    return ctx, sb, sem


def prepare(nc, t, k, bank, wide):
    ctx, sb, sem = phase(nc)
    with ctx:
        zero = sb("zero", [P, ZROWS * AGG0])
        tri = sb("tri", [P, P])
        count_i = sb("count_i", [P, 1], I32)
        own = sb("own", [P, 1])
        stage = sb("stage", [P, 1600])
        ids = sb("ids", [P, 4, P], I32)
        idf = sb("idf", [P, 4, P])
        srcf = sb("srcf", [P, TILES])
        dstf = sb("dstf", [P, TILES])
        spread = sb("spread", [P, 2, 2, P])
        of = sb("of", [VC, C])
        below = sb("below", [P, 2, P])
        earlier = sb("earlier", [P, TILES])
        s_zero, s_zeroed = sem("s_zero"), sem("s_zeroed")
        s_in, s_ids, s_const, s_own = sem("s_in"), sem("s_ids"), sem("s_const"), sem("s_own")
        s_idf, s_turned, s_ids_up = sem("s_idf"), sem("s_turned"), sem("s_ids_up")
        s_spread, s_rows, s_same, s_below, s_red, s_dve = (
            sem("s_spread"), sem("s_rows"), sem("s_same"), sem("s_below"), sem("s_red"), sem("s_dve"))
        half = TILES // 2
        parts = [("src", 0), ("dst", 2)]
        loads = []

        def load(name, r0, r1, p0, c0):
            cols = t[name].shape[1]
            loads.append((stage[p0:p0 + r1 - r0, c0:c0 + cols], t[name][r0:r1, :]))
            return stage[p0:p0 + r1 - r0, c0:c0 + cols]

        c = [0]

        def at(width):
            c[0] += width
            return c[0] - width

        def thrice(name, r0=0):
            a = at(t[name].shape[1])
            return [load(name, r0, r0 + V, V * i, a) for i in range(C)]

        def woven(name):
            a = at(V)
            for i in range(C):
                loads.append((stage[i:VC:C, a:a + V], t[name][:, :]))
            return stage[0:VC, a:a + V]

        wl10, wsc0 = load("L0_gnn_Wl1_0", 0, S, 0, at(64)), load("L0_gnn_Wsc0", 0, S, 0, at(64))
        wl11, wsc1 = woven("L0_gnn_Wl1_1"), woven("L0_gnn_Wsc1")
        wfc1, wfc2 = load("L0_gnn_Wfc1", 0, 8, 0, at(64)), load("L0_gnn_Wfc2", 0, 64, 0, at(64))
        wfc3 = load("L0_gnn_Wfc3", 0, 64, 0, at(W0N))
        x = at(64)
        l2s_a, l2s_b = load("L0_gnn_Wl2_s", 0, 64, 64, x), load("L0_gnn_Wl2_s", 64, 96, 96, at(64))
        x = at(1)
        wa_a, wa_b = load("L0_gnn_Wa", 0, 64, 64, x), load("L0_gnn_Wa", 64, 96, 96, at(1))
        l2v_a, l2v_b = load("L0_gnn_Wl2_v", 0, 64, 0, at(32)), thrice("L0_gnn_Wl2_v", 64)
        gws, gwv = load("L1_gnn_lin1_ws", 0, S, 0, at(64)), woven("L1_gnn_lin1_wv")
        gf1, gf2 = load("L1_gnn_fc_w1", 0, 64, 0, at(64)), load("L1_gnn_fc_w2", 0, 64, 0, at(W1N))
        x = at(96)
        m2s_a, m2s_b = load("L1_gnn_lin2_ws", 0, 64, 64, x), load("L1_gnn_lin2_ws", 64, 96, 96, at(96))
        m2v_a = load("L1_gnn_lin2_wv", 0, 64, 0, at(32))
        m2v_b, m2v_c = thrice("L1_gnn_lin2_wv", 64), thrice("L1_gnn_lin2_wv", 96)
        gscs, gscv = load("L1_gnn_sc_ws", 0, S, 0, at(96)), woven("L1_gnn_sc_wv")
        assert c[0] <= 1600
        n_in = 16 * len(loads)

        with nc.Block() as block:

            @block.sync
            def _(sp):
                for name, at_ in parts:
                    full = t[name][0:(TILES - 1) * P].rearrange("(t p) -> t p", p=P)
                    if at_ == 0:
                        sp.wait_ge(s_ids, 1)
                    sp.dma_start(ids[0:half, at_, :], full[0:half, :]).then_inc(s_ids_up, 16)
                    sp.dma_start(ids[0:half - 1, at_ + 1, :], full[half:2 * half - 1, :]).then_inc(s_ids_up, 16)
                    sp.dma_start(ids[half - 1:half, at_ + 1, 0:TAIL],
                                 t[name][(TILES - 1) * P:EDGES].rearrange("(t p) -> t p", t=1)).then_inc(s_ids_up, 16)
                for dst, src in loads:
                    sp.dma_start(dst, src).then_inc(s_in, 16)
                table = t["agg0"].rearrange("(p r) c -> p (r c)", p=P)
                sp.wait_ge(s_zero, 1)
                with sp.Fori(0, NZ) as i:
                    sp.dma_start(table[:, bass.ds(i * (ZROWS * AGG0), ZROWS * AGG0)], zero[:, :]).then_inc(s_zeroed, 16)
                sp.wait_ge(s_zeroed, 16 * NZ)

            @block.gpsimd
            def _(pool):
                pool.memset(ids[:, 0:2, :], 0)
                pool.memset(ids[:, 2:4, :], NODES).then_inc(s_ids, 1)
                pool.memset(zero[:, :], 0.0).then_inc(s_zero, 1)
                pool.memset(k["ident"][:, :], 1.0)
                pool.memset(tri[:, :], 1.0).then_inc(s_const, 1)
                pool.wait_ge(s_const, 1)
                pool.affine_select(out=k["ident"][:, :], in_=k["ident"][:, :], compare_op=ALU.is_equal, fill=0.0,
                                   base=0, pattern=[[-1, P]], channel_multiplier=1).then_inc(s_const, 1)
                pool.affine_select(out=tri[:, :], in_=tri[:, :], compare_op=ALU.is_gt, fill=0.0, base=0,
                                   pattern=[[-1, P]], channel_multiplier=1).then_inc(s_const, 1)
                pool.iota(count_i[:, :], pattern=[[0, 1]], base=SPARE, channel_multiplier=1).then_inc(s_own, 1)

            @block.tensor
            def _(pe):
                pe.wait_ge(s_const, 3)
                pe.wait_ge(s_idf, 1)
                for j in range(4):
                    ins = pe.transpose(bank[0][:, j * P:j * P + half], idf[0:half, j, :], k["ident"][0:half, 0:half])
                ins.then_inc(s_turned, 1)

                def turn(q):
                    pe.wait_ge(s_spread, q.g + 1)
                    if not (isinstance(q.g, int) and q.g < 1):
                        pe.wait_ge(s_same, q.g)
                    for j in range(2):
                        ins = pe.transpose(bank[1][:, j * P:j * P + P], spread[:, q.h, j, :], k["ident"][:, :])
                    ins.then_inc(s_rows, 1)

                passes(pe, PAIRS, [(0, turn)])

            @block.vector
            def _(dve):
                done = [0]

                def link(ins):
                    done[0] += 1
                    ins.then_inc(s_dve, 1)
                    dve.wait_ge(s_dve, done[0])

                def scaled(out, in_, scale):
                    return dve.tensor_scalar(out, in_, float(scale), None, ALU.mult)

                dve.wait_ge(s_ids_up, 96)
                dve.tensor_copy(idf[:, :, :], ids[:, :, :]).then_inc(s_idf, 1)
                dve.wait_ge(s_own, 1)
                dve.tensor_copy(own[:, :], count_i[:, :])
                for name in ("w0v", "out0a", "out0b", "w1v", "out1a", "out1b", "out1c", "sc1v"):
                    dve.memset(k[name][:, :], 0.0)
                dve.wait_ge(s_turned, 1)
                for m, to in ((0, srcf), (2, dstf)):
                    for j in range(2):
                        ins = dve.tensor_copy(to[:, j * half:(j + 1) * half], bank[0][:, (m + j) * P:(m + j) * P + half])
                link(ins)
                dve.tensor_copy(k["src"][:, :], srcf[:, :])

                def spread_dst(q):
                    if not (isinstance(q.g, int) and q.g < 2):
                        dve.wait_ge(s_rows, q.g - 1)
                    v = dstf[:, bass.ds(q.g * 2, 2)].unsqueeze(2).to_broadcast([P, 2, P])
                    dve.tensor_copy(spread[:, q.h, :, :], v).then_inc(s_spread, 1)

                def compare(q):
                    dve.wait_ge(s_rows, q.g + 1)
                    for j in range(2):
                        ins = dve.tensor_scalar(k["same"][:, bass.ds(q.g * 2 + j, 1), :].rearrange("p a b -> p (a b)"), bank[1][:, j * P:j * P + P],
                                                dstf[:, bass.ds(q.g * 2 + j, 1)], None, ALU.is_equal)
                    ins.then_inc(s_same, 1)
                    dve.wait_ge(s_same, q.g + 1)
                    tri2 = tri[:, :].unsqueeze(1).to_broadcast([P, 2, P])
                    dve.tensor_tensor(below[:, :, :], k["same"][:, bass.ds(q.g * 2, 2), :], tri2,
                                      ALU.mult).then_inc(s_below, 1)
                    dve.wait_ge(s_below, q.g + 1)
                    link_free = dve.tensor_reduce(earlier[:, bass.ds(q.g * 2, 2)], below[:, :, :], AX.X, ALU.add)
                    link_free.then_inc(s_red, 1)
                    dve.wait_ge(s_red, q.g + 1)

                dve.wait_ge(s_const, 3)
                passes(dve, PAIRS, [(1, spread_dst), (0, compare)])

                link(dve.tensor_scalar(earlier[:, :], earlier[:, :], 0.0, None, ALU.is_gt))
                link(dve.tensor_scalar(srcf[:, :], dstf[:, :], -1.0, own[:, 0:1], ALU.mult, ALU.add))
                link(dve.tensor_tensor(srcf[:, :], srcf[:, :], earlier[:, :], ALU.mult))
                link(dve.tensor_tensor(dstf[:, :], dstf[:, :], srcf[:, :], ALU.add))
                link(dve.tensor_copy(k["row"][:, :], dstf[:, :]))

                dve.wait_ge(s_in, n_in)
                scaled(k["w0s"][:, 0:S], wl10, 1 / 8)
                scaled(k["w0s"][:, S:2 * S], wsc0, 1 / 8)
                scaled(k["fc1"][:, :], wfc1, 8 ** -0.5)
                scaled(k["fc2"][:, :], wfc2, 1 / 8)
                scaled(k["fc3"][:, 0:64], wfc3[:, 64:128], 1 / 8)
                scaled(k["fc3"][:, 64:96], wfc3[:, 160:192], 1 / 8)
                scaled(k["fc3"][:, 96:160], wfc3[:, 0:64], 1 / 8)
                scaled(k["fc3"][:, 160:192], wfc3[:, 128:160], 1 / 8)
                n0 = 32 ** -0.5 * 96 ** -0.5
                scaled(k["out0a"][0:64, AGG0:MSG0], l2v_a, n0)
                scaled(k["out0a"][64:128, 0:64], l2s_a, n0)
                scaled(k["out0a"][64:128, 64:65], wa_a, n0)
                scaled(k["out0b"][96:128, 0:64], l2s_b, n0 * 3 ** -0.5)
                scaled(k["out0b"][96:128, 64:65], wa_b, n0 * 3 ** -0.5)
                scaled(k["w1s"][:, :], gws, 1 / 8)
                scaled(k["gfc1"][:, :], gf1, 1 / 8)
                for to, c0, n in ((0, 64, 64), (64, 160, 32), (96, 192, 32), (128, 0, 64), (192, 128, 32)):
                    scaled(k["gfc2"][:, to:to + n], gf2[:, c0:c0 + n], 1 / 8)
                n1s, n1v = 0.25 * 96 ** -0.5, 0.25 * 128 ** -0.5
                scaled(k["out1a"][0:64, AGG1:MSG1], m2v_a, n1v)
                scaled(k["out1a"][64:128, 0:96], m2s_a, n1s)
                scaled(k["out1b"][96:128, 0:96], m2s_b, n1s * 3 ** -0.5)
                scaled(k["sc1s"][:, :], gscs, 1 / 8)
                for i in range(C):
                    ins = dve.tensor_reduce(of[:, i:i + 1], k["ident"][0:VC, i:VC:C], AX.X, ALU.add)
                link(ins)
                link(scaled(of[:, :], of[:, :], 32 ** -0.5))
                for i in range(C):
                    p = slice(V * i, V * i + V)

                    def component(out, in_):
                        dve.tensor_scalar(out, in_, of[:, i:i + 1], None, ALU.mult)

                    component(k["w0v"][:, i:VC:C], wsc1)
                    component(k["sc1v"][:, i:VC:C], gscv)
                    component(k["w0v"][:, VC + V * i:VC + V * i + V], wl11)
                    component(k["w1v"][:, V * i:V * i + V], gwv)
                    if i < 2:
                        component(k["w1v"][:, V * (i + 3):V * (i + 3) + V], gwv)
                    scaled(k["out0b"][p, 65 + V * i:65 + V * i + V], l2v_b[i], n0)
                    scaled(k["out1b"][p, 96 + V * i:96 + V * i + V], m2v_b[i], n1v)
                    scaled(k["out1c"][p, V * i:V * i + V], m2v_c[i], n1v * 2 ** -0.5)
                dve.drain()


def edges0(nc, t, k, bank, wide):
    ctx, sb, sem = phase(nc)
    with ctx:
        zero = sb("zero1", [P, ZROWS * AGG1])
        xs = sb("xs", [P, 2, 2, FEAT])
        idx = sb("idx", [P, 2, 2], I32)
        rows = sb("rows", [P, 2, 2], I32)
        a = sb("a", [P, 2, 2])
        e4 = sb("e4", [P, 2, 2, 4])
        e8 = sb("e8", [P, 2, 2, 8])
        ay = sb("ay", [P, 2, 2, 4])
        xT = sb("xT", [VC, 2, 2, P])
        eT = sb("eT", [8, 2, P])
        h1 = sb("h1", [64, 2 * P])
        h2 = sb("h2", [64, 2 * P])
        w = sb("w", [P, 2, 2, 96])
        dot = sb("dot", [P, 2, C, V])
        dots = sb("dots", [P, 2, V])
        mid = sb("mid", [P, 2, 2, P])
        midT = sb("midT", [P, 2, 2, P])
        yb = sb("yb", [P, 2, 2, FEAT])
        qy = sb("qy", [P, 2, C, V])
        msg = sb("msg", [P, 2, AGG0])
        eq = sb("eq", [P, 2, P])
        total = sb("total", [P, 2, 2, AGG0])
        xTp, hp, wp, midTp, msgp, sump = bank
        xTp4 = xTp[:, :].rearrange("p (j s e) -> p j s e", j=2, s=2)
        midTp4 = midTp[:, :].rearrange("p (j s e) -> p j s e", j=2, s=2)
        wp3 = wp[:, 0:2 * W0N].rearrange("p (j n) -> p j n", j=2)
        msgp3 = msgp[:, 0:2 * MSG0].rearrange("p (j n) -> p j n", j=2)
        sump3 = sump[:, 0:2 * AGG0].rearrange("p (j n) -> p j n", j=2)
        names = ("passed z zd pad idx gx0 gx1 e_in0 e_in1 xTp xT f fw ay wp w01 w23 m1 m3 dot dots midTp midT msgp msgs "
                 "msg eqs sump total0 rows sc00 sc01 sc10 sc11 eTp eT h1p h1 h2p h2 yb ybo0 ybo1 qy").split()
        s = {n: sem("e0_" + n) for n in names}

        def first(q, n):
            return isinstance(q.g, int) and q.g < n

        def last(q):
            return isinstance(q.g, int) and q.g == PAIRS - 1

        def plain(engine):
            engine.sem_inc(s["passed"], 1)

        with nc.Block() as block:

            @block.sync
            def _(sp):
                zt = t["agg1"].rearrange("(p r) c -> p (r c)", p=P)

                def load(q):
                    if not first(q, 2):
                        sp.wait_ge(s["ay"], q.g - 1)
                        sp.wait_ge(s["eTp"], q.g - 1)
                    if last(q):
                        sp.wait_ge(s["pad"], 1)
                    for name, to in (("edge_attr_4", e4), ("edge_attr_8", e8)):
                        if last(q):
                            e = 2 * (PAIRS - 1) * P
                            sp.dma_start(to[:, q.h, 0, :], t[name][e:e + P, :]).then_inc(s[f"e_in{q.h}"], 16)
                            sp.dma_start(to[0:TAIL, q.h, 1, :], t[name][e + P:EDGES, :]).then_inc(s[f"e_in{q.h}"], 16)
                        else:
                            v = t[name][bass.ds(q.g * (2 * P), 2 * P), :].rearrange("(j p) c -> p j c", j=2)
                            sp.dma_start(to[:, q.h, :, :], v).then_inc(s[f"e_in{q.h}"], 16)

                def clear(q):
                    sp.dma_start(zt[:, bass.ds(q.g * (ZROWS * AGG1), ZROWS * AGG1)], zero[:, :]).then_inc(s["zd"], 16)

                def store(q):
                    sp.wait_ge(s["yb"], q.g + 1)
                    sp.dma_start(t["ybase"][bass.ds(q.g, 1)].rearrange("g p j c -> (g p) j c"), yb[:, q.h, :, :]).then_inc(s[f"ybo{q.h}"], 16)

                sp.wait_ge(s["z"], 1)
                passes(sp, PAIRS, [(3, load), (0, clear), (1, store)])
                sp.wait_ge(s["zd"], 16 * NZ)
                sp.wait_ge(s["ybo0"], 16 * (PAIRS // 2))
                sp.wait_ge(s["ybo1"], 16 * (PAIRS // 2))

            @block.gpsimd
            def _(pool):
                pool.memset(zero[:, :], 0.0).then_inc(s["z"], 1)

                def gather(q):
                    if not first(q, 2):
                        pool.wait_ge(s[f"gx{q.h}"], q.u * 64)
                        pool.wait_ge(s["yb"], q.g - 1)
                        pool.wait_ge(s["xTp"], q.g - 1)
                    pool.tensor_copy(idx[:, q.h, :], k["src"][:, bass.ds(q.g * 2, 2)]).then_inc(s["idx"], 1)
                    pool.wait_ge(s["idx"], q.g + 1)
                    plain(pool)
                    for j in range(2):
                        at = bass.IndirectOffsetOnAxis(ap=idx[:, q.h, j:j + 1], axis=0)
                        pool.indirect_dma_start(xs[:, q.h, j, :], None, t["x"], at).then_inc(s[f"gx{q.h}"], 16)
                        pool.indirect_dma_start(a[:, q.h, j:j + 1], None, t["node_vec1"], at).then_inc(s[f"gx{q.h}"], 16)

                def pad(q):
                    if last(q):
                        pool.wait_ge(s["ay"], q.g - 1)
                        pool.memset(e4[:, q.h, 1, :], 0.0).then_inc(s["pad"], 1)

                def scatter(j):
                    def of(q):
                        if j == 0:
                            pool.tensor_copy(rows[:, q.h, :], k["row"][:, bass.ds(q.g * 2, 2)]).then_inc(s["rows"], 1)
                            pool.wait_ge(s["rows"], q.g + 1)
                            pool.wait_ge(s["total0"], q.g + 1)
                            if not first(q, 1):
                                pool.wait_ge(s[f"sc{1 - q.h}1"], (q.u + q.h) * 16)
                        else:
                            pool.wait_ge(s[f"sc{q.h}0"], (q.u + 1) * 16)
                        plain(pool)
                        at = bass.IndirectOffsetOnAxis(ap=rows[:, q.h, j:j + 1], axis=0)
                        pool.indirect_dma_start(t["agg0"], at, total[:, q.h, j, :], None,
                                                compute_op=ALU.add).then_inc(s[f"sc{q.h}{j}"], 16)
                    return of

                passes(pool, PAIRS, [(2, pad), (-1, scatter(0)), (3, gather), (-1, scatter(1))])
                for n in ("sc00", "sc01", "sc10", "sc11"):
                    pool.wait_ge(s[n], 16 * (PAIRS // 2))

            @block.tensor
            def _(pe):
                ident = k["ident"]

                def turn(q):
                    pe.wait_ge(s[f"gx{q.h}"], (q.u + 1) * 64)
                    if not first(q, 1):
                        pe.wait_ge(s["xT"], q.g)
                    for j in range(2):
                        pe.transpose(xTp4[0:VC, j, 0, :], xs[:, q.h, j, 0:VC], ident[:, :])
                        ins = pe.transpose(xTp4[0:VC, j, 1, :], xs[:, q.h, j, S:FEAT], ident[:, :])
                    ins.then_inc(s["xTp"], 1)

                def turn_edges(q):
                    pe.wait_ge(s[f"e_in{q.h}"], (q.u + 1) * 32 + 32 * last(q))
                    if not first(q, 1):
                        pe.wait_ge(s["h2"], q.g)
                    for j in range(2):
                        ins = pe.transpose(hp[0:8, j * P:j * P + P], e8[:, q.h, j, :], ident[:, :])
                    ins.then_inc(s["eTp"], 1)

                def linear(q):
                    pe.wait_ge(s["xT"], q.g + 1)
                    if not first(q, 1):
                        pe.wait_ge(s["fw"], q.g)
                        pe.wait_ge(s["m1"], q.g)
                        pe.wait_ge(s["yb"], q.g)
                    for j in range(2):
                        pe.matmul(wide[:, j, 0:2 * S], xT[0:S, j, 0, :], k["w0s"][:, :], start=True, stop=True)
                        ins = pe.matmul(wide[:, j, 2 * S:2 * FEAT], xT[:, j, 1, :], k["w0v"][:, :], start=True, stop=True)
                    ins.then_inc(s["f"], 1)

                def network1(q):
                    pe.wait_ge(s["eT"], q.g + 1)
                    pe.matmul(hp[0:64, 0:2 * P], k["fc1"][:, :], eT[:, :, :].rearrange("c j e -> c (j e)"),
                              start=True, stop=True).then_inc(s["h1p"], 1)

                def network2(q):
                    pe.wait_ge(s["h1"], q.g + 1)
                    plain(pe)
                    pe.matmul(hp[0:64, 2 * P:4 * P], k["fc2"][:, :], h1[:, :], start=True, stop=True).then_inc(s["h2p"], 1)

                def network3(q):
                    pe.wait_ge(s["h2"], q.g + 1)
                    if not first(q, 1):
                        pe.wait_ge(s["w01"], q.g)
                        pe.wait_ge(s["w23"], q.g)
                    for j in range(2):
                        ins = pe.matmul(wp3[:, j, :], h2[:, j * P:j * P + P], k["fc3"][:, :], start=True, stop=True)
                    ins.then_inc(s["wp"], 1)

                def turn_mid(q):
                    for n in ("m1", "fw", "m3"):
                        pe.wait_ge(s[n], q.g + 1)
                    if not first(q, 1):
                        pe.wait_ge(s["midT"], q.g)
                    for j in range(2):
                        for m in range(2):
                            ins = pe.transpose(midTp4[:, j, m, :], mid[:, j, m, :], ident[:, :])
                    ins.then_inc(s["midTp"], 1)

                def out(q):
                    pe.wait_ge(s["midT"], q.g + 1)
                    if not first(q, 1):
                        pe.wait_ge(s["msgs"], q.g)
                        pe.wait_ge(s["msg"], q.g)
                    for j in range(2):
                        pe.matmul(msgp3[:, j, :], midT[:, j, 0, :], k["out0a"][:, :], start=True, stop=False)
                        ins = pe.matmul(msgp3[:, j, 0:AGG0], midT[:, j, 1, :], k["out0b"][:, :], start=False, stop=True)
                    ins.then_inc(s["msgp"], 1)

                def add_up(q):
                    pe.wait_ge(s["msgs"], q.g + 1)
                    pe.wait_ge(s["msg"], q.g + 1)
                    pe.wait_ge(s["eqs"], q.g + 1)
                    if not first(q, 1):
                        pe.wait_ge(s["total0"], q.g)
                    for j in range(2):
                        ins = pe.matmul(sump3[:, j, :], eq[:, j, :], msg[:, j, :], start=True, stop=True)
                    ins.then_inc(s["sump"], 1)

                passes(pe, PAIRS, [(1, linear), (2, turn_edges), (-1, add_up), (0, turn_mid), (2, network1), (2, turn),
                                   (2, network2), (0, out), (2, network3)])

            @block.scalar
            def _(act):
                def turned(q):
                    act.wait_ge(s["xTp"], q.g + 1)
                    if not first(q, 1):
                        act.wait_ge(s["f"], q.g)
                    act.copy(xT[:, :, :, :], xTp4[0:VC, :, :, :]).then_inc(s["xT"], 1)

                def edges_turned(q):
                    act.wait_ge(s["eTp"], q.g + 1)
                    if not first(q, 1):
                        act.wait_ge(s["h1p"], q.g)
                    act.copy(eT[:, :, :].rearrange("c j e -> c (j e)"), hp[0:8, 0:2 * P]).then_inc(s["eT"], 1)

                def network1(q):
                    act.wait_ge(s["h1p"], q.g + 1)
                    if not first(q, 1):
                        act.wait_ge(s["h2p"], q.g)
                    act.activation(h1[:, :], hp[0:64, 0:2 * P], ACT.Gelu_apprx_tanh).then_inc(s["h1"], 1)

                def network2(q):
                    act.wait_ge(s["h2p"], q.g + 1)
                    if not first(q, 1):
                        act.wait_ge(s["wp"], q.g)
                    act.activation(h2[:, :], hp[0:64, 2 * P:4 * P], ACT.Gelu_apprx_tanh).then_inc(s["h2"], 1)

                def weights(q):
                    act.wait_ge(s["wp"], q.g + 1)
                    if not first(q, 1):
                        for n in ("m1", "fw", "m3"):
                            act.wait_ge(s[n], q.g)
                    act.copy(w[:, 0, :, :], wp3[:, :, 0:96]).then_inc(s["w01"], 1)

                def mid_turned(q):
                    act.wait_ge(s["midTp"], q.g + 1)
                    if not first(q, 1):
                        act.wait_ge(s["msgp"], q.g)
                    act.copy(midT[:, :, :, :], midTp4[:, :, :, :]).then_inc(s["midT"], 1)

                def scalars_out(q):
                    act.wait_ge(s["msgp"], q.g + 1)
                    if not first(q, 1):
                        act.wait_ge(s["sump"], q.g)
                    act.copy(msg[:, :, 0:S], msgp3[:, :, 0:S])
                    act.copy(msg[:, :, FEAT:AGG0], msgp3[:, :, S:S + 1]).then_inc(s["msgs"], 1)

                def summed(q):
                    act.wait_ge(s["sump"], q.g + 1)
                    if not first(q, 2):
                        act.wait_ge(s[f"sc{q.h}0"], q.u * 16)
                        act.wait_ge(s[f"sc{q.h}1"], q.u * 16)
                    act.copy(total[:, q.h, :, :], sump3[:, :, :]).then_inc(s["total0"], 1)

                def equal(q):
                    if not first(q, 1):
                        act.wait_ge(s["sump"], q.g)
                    act.copy(eq[:, :, :], k["same"][:, bass.ds(q.g * 2, 2), :]).then_inc(s["eqs"], 1)

                passes(act, PAIRS, [(1, weights), (2, edges_turned), (-1, summed), (0, mid_turned), (2, network1),
                                    (2, turned), (2, network2), (0, scalars_out), (0, equal)])

            @block.vector
            def _(dve):
                def attributes(q):
                    dve.wait_ge(s[f"gx{q.h}"], (q.u + 1) * 64)
                    dve.wait_ge(s[f"e_in{q.h}"], (q.u + 1) * 32 + 32 * last(q))
                    if not first(q, 2):
                        dve.wait_ge(s["msg"], q.g - 1)
                    dve.tensor_tensor(ay[:, q.h, :, :], e4[:, q.h, :, :], a[:, q.h, :].unsqueeze(2).to_broadcast([P, 2, 4]),
                                      ALU.mult).then_inc(s["ay"], 1)
                    dve.tensor_copy(k["a_src"][:, bass.ds(q.g * 2, 2)], a[:, q.h, :])

                def product(q):
                    y0 = ay[:, q.h, :, 0:1].to_broadcast([P, 2, 96])
                    y1 = ay[:, q.h, :, 1:4].unsqueeze(3).to_broadcast([P, 2, C, V])
                    fs = wide[:, :, 0:S].unsqueeze(2).to_broadcast([P, 2, 2, S])
                    fv = wide[:, :, 2 * S + VC:2 * FEAT].rearrange("p j (c u) -> p j c u", c=C)
                    dve.wait_ge(s["ay"], q.g + 1)
                    dve.wait_ge(s["f"], q.g + 1)
                    if not first(q, 2):
                        dve.wait_ge(s[f"ybo{q.h}"], q.u * 16)
                    dve.tensor_tensor(dot[:, :, :, :], fv, y1, ALU.mult).then_inc(s["dot"], 1)
                    for j in range(2):
                        ins = dve.scalar_tensor_tensor(yb[:, q.h, j, :], wide[:, j, S:S + FEAT], a[:, q.h, j:j + 1],
                                                       xs[:, q.h, j, :], ALU.mult, ALU.add)
                    ins.then_inc(s["yb"], 1)
                    dve.wait_ge(s["dot"], q.g + 1)
                    dve.tensor_reduce(dots[:, :, :], dot[:, :, :, :].rearrange("p j c u -> p j u c"), AX.X,
                                      ALU.add).then_inc(s["dots"], 1)
                    dve.wait_ge(s["w01"], q.g + 1)
                    dve.tensor_tensor(w[:, 1, :, :], wp3[:, :, 96:192], y0, ALU.mult).then_inc(s["w23"], 1)
                    dve.wait_ge(s["w23"], q.g + 1)
                    if not first(q, 1):
                        dve.wait_ge(s["midTp"], q.g)
                    w10 = w[:, :, :, 0:S].rearrange("p m j n -> p j m n")
                    dve.tensor_tensor(mid[:, :, 0, :].rearrange("p j (m n) -> p j m n", m=2), w10, fs, ALU.mult).then_inc(s["m1"], 1)
                    dve.tensor_tensor(mid[:, :, 1, 0:VC].rearrange("p j (c u) -> p j c u", c=C), fv,
                                      w[:, 1, :, 64:96].unsqueeze(2).to_broadcast([P, 2, C, V]), ALU.mult).then_inc(s["fw"], 1)
                    dve.wait_ge(s["dots"], q.g + 1)
                    dve.tensor_tensor(mid[:, :, 1, VC:P], dots[:, :, :], w[:, 0, :, 64:96], ALU.mult).then_inc(s["m3"], 1)

                def vectors_out(q):
                    dve.wait_ge(s["msgs"], q.g + 1)
                    y1 = ay[:, q.h, :, 1:4].unsqueeze(3).to_broadcast([P, 2, C, V])
                    qv = msgp3[:, :, AGG0:MSG0].unsqueeze(2).to_broadcast([P, 2, C, V])
                    dve.tensor_tensor(qy[:, :, :, :], qv, y1, ALU.mult).then_inc(s["qy"], 1)
                    dve.wait_ge(s["qy"], q.g + 1)
                    if not first(q, 1):
                        dve.wait_ge(s["sump"], q.g)
                    dve.tensor_tensor(msg[:, :, S:FEAT].rearrange("p j (u c) -> p j c u", c=C), qy[:, :, :, :],
                                      msgp3[:, :, S + 1:AGG0].rearrange("p j (c u) -> p j c u", c=C),
                                      ALU.add).then_inc(s["msg"], 1)

                passes(dve, PAIRS, [(1, attributes), (1, product), (0, vectors_out)])
                dve.drain()


def edges1(nc, t, k, bank, wide):
    ctx, sb, sem = phase(nc)
    with ctx:
        yb = sb("g_yb", [P, 2, 2, FEAT])
        agg = sb("g_agg", [P, 2, 2, AGG0])
        idx = sb("g_idx", [P, 2, 2], I32)
        rows = sb("g_rows", [P, 2, 2], I32)
        a2 = sb("g_a2", [P, TILES])
        half = sb("g_half", [P, 2])
        e4 = sb("g_e4", [P, 2, 2, 4])
        e64 = sb("g_e64", [P, 2, 2, 64])
        ye = sb("g_ye", [P, 2, 2, 6])
        al = sb("g_al", [P, 2])
        y = sb("g_y", [P, 2, 2, FEAT])
        stats = sb("g_stats", [P, 2, 6])
        mv = sb("g_mv", [P, 2, 2, 2])
        var = sb("g_var", [P, 2])
        rstd = sb("g_rstd", [P, 2])
        ra = sb("g_ra", [P, 2])
        x1 = sb("g_x1", [P, 2, 2, FEAT])
        xT = sb("g_xT", [VC, 2, 2, P])
        eT = sb("g_eT", [64, 2 * P])
        hid = sb("g_hid", [64, 2 * P])
        w = sb("g_w", [P, 2, 2, P])
        dot = sb("g_dot", [P, 2, C, V])
        dots = sb("g_dots", [P, 2, V])
        ca = sb("g_ca", [P, 2, C, V])
        cb = sb("g_cb", [P, 2, C, V])
        cc = sb("g_cc", [P, 2, C, V])
        mid = sb("g_mid", [P, 2, 2, P])
        mid3 = sb("g_mid3", [P, 2, VC])
        midT = sb("g_midT", [P, 2, 2, P])
        mid3T = sb("g_mid3T", [VC, 2, P])
        qy = sb("g_qy", [P, 2, C, V])
        msg = sb("g_msg", [P, 2, AGG1])
        eq = sb("g_eq", [P, 2, P])
        total = sb("g_total", [P, 2, 2, AGG1])
        xTp, hp, wp, midTp, msgp, sump = bank
        xTp4 = xTp[:, :].rearrange("p (j s e) -> p j s e", j=2, s=2)
        midTp4 = midTp[:, :].rearrange("p (j s e) -> p j s e", j=2, s=2)
        wp3 = wp[:, 0:2 * W1N].rearrange("p (j n) -> p j n", j=2)
        HW = S + 5 * V
        hvp = wide[:, 0, 0:2 * HW].rearrange("p (j n) -> p j n", j=2)
        mid3Tp = wide[:, 1, 0:2 * P].rearrange("p (j e) -> p j e", j=2)
        msgp3 = msgp[:, 0:2 * MSG1].rearrange("p (j n) -> p j n", j=2)
        sump3 = sump[:, 0:2 * AGG1].rearrange("p (j n) -> p j n", j=2)
        names = ("passed half a2 idx in0 in1 yin0 yin1 ein0 ein1 pad al y st mv var rstd ra x1 ye xTp eTp xT eT f h1p h1 wp wa wb m0 m1 "
                 "dot dots m2 ca cc m3 midTp mid3Tp midT mid3T msgp msgs msg qy eqs sump total0 rows sc00 sc01 sc10 sc11").split()
        s = {n: sem("e1_" + n) for n in names}

        def first(q, n):
            return isinstance(q.g, int) and q.g < n

        def last(q):
            return isinstance(q.g, int) and q.g == PAIRS - 1

        def plain(engine):
            engine.sem_inc(s["passed"], 1)

        with nc.Block() as block:

            @block.sync
            def _(sp):
                def load(q):
                    if not first(q, 2):
                        sp.wait_ge(s["y"], q.g - 1)
                    sp.dma_start(yb[:, q.h, :, :], t["ybase"][bass.ds(q.g, 1)].rearrange("g p j c -> (g p) j c")).then_inc(s[f"yin{q.h}"], 16)

                def load_edges(q):
                    if not first(q, 2):
                        sp.wait_ge(s["ye"], q.g - 1)
                        sp.wait_ge(s["eTp"], q.g - 1)
                    if last(q):
                        sp.wait_ge(s["pad"], 1)
                    for name, to in (("edge_attr_4", e4), ("edge_attr_64", e64)):
                        if last(q):
                            e = 2 * (PAIRS - 1) * P
                            sp.dma_start(to[:, q.h, 0, :], t[name][e:e + P, :]).then_inc(s[f"ein{q.h}"], 16)
                            sp.dma_start(to[0:TAIL, q.h, 1, :], t[name][e + P:EDGES, :]).then_inc(s[f"ein{q.h}"], 16)
                        else:
                            v = t[name][bass.ds(q.g * (2 * P), 2 * P), :].rearrange("(j p) c -> p j c", j=2)
                            sp.dma_start(to[:, q.h, :, :], v).then_inc(s[f"ein{q.h}"], 16)

                passes(sp, PAIRS, [(4, load), (3, load_edges)])

            @block.gpsimd
            def _(pool):
                pool.memset(half[:, :], -0.5).then_inc(s["half"], 1)
                pool.wait_ge(s["half"], 1)

                def gather(q):
                    if not first(q, 2):
                        pool.wait_ge(s[f"in{q.h}"], q.u * 32)
                        pool.wait_ge(s["y"], q.g - 1)
                    pool.tensor_copy(idx[:, q.h, :], k["src"][:, bass.ds(q.g * 2, 2)]).then_inc(s["idx"], 1)
                    pool.wait_ge(s["idx"], q.g + 1)
                    plain(pool)
                    for j in range(2):
                        at = bass.IndirectOffsetOnAxis(ap=idx[:, q.h, j:j + 1], axis=0)
                        pool.indirect_dma_start(agg[:, q.h, j, :], None, t["agg0"], at).then_inc(s[f"in{q.h}"], 16)

                def pad(q):
                    if last(q):
                        pool.wait_ge(s["ye"], q.g - 1)
                        pool.memset(e4[:, q.h, 1, :], 0.0).then_inc(s["pad"], 1)

                def root(q):
                    pool.wait_ge(s["var"], q.g + 1)
                    if not first(q, 1):
                        pool.wait_ge(s["ra"], q.g)
                    pool.tensor_tensor(rstd[:, :], var[:, :], half[:, :], ALU.pow).then_inc(s["rstd"], 1)

                def scatter(j):
                    def of(q):
                        if j == 0:
                            pool.tensor_copy(rows[:, q.h, :], k["row"][:, bass.ds(q.g * 2, 2)]).then_inc(s["rows"], 1)
                            pool.wait_ge(s["rows"], q.g + 1)
                            pool.wait_ge(s["total0"], q.g + 1)
                            if not first(q, 1):
                                pool.wait_ge(s[f"sc{1 - q.h}1"], (q.u + q.h) * 16)
                        else:
                            pool.wait_ge(s[f"sc{q.h}0"], (q.u + 1) * 16)
                        plain(pool)
                        at = bass.IndirectOffsetOnAxis(ap=rows[:, q.h, j:j + 1], axis=0)
                        pool.indirect_dma_start(t["agg1"], at, total[:, q.h, j, :], None,
                                                compute_op=ALU.add).then_inc(s[f"sc{q.h}{j}"], 16)
                    return of

                passes(pool, PAIRS, [(2, pad), (-1, scatter(0)), (4, gather), (-1, scatter(1)), (3, root)])
                for n in ("sc00", "sc01", "sc10", "sc11"):
                    pool.wait_ge(s[n], 16 * (PAIRS // 2))

            @block.tensor
            def _(pe):
                ident = k["ident"]

                def turn(q):
                    pe.wait_ge(s["x1"], q.g + 1)
                    if not first(q, 1):
                        pe.wait_ge(s["xT"], q.g)
                    for j in range(2):
                        pe.transpose(xTp4[0:VC, j, 0, :], x1[:, q.h, j, 0:VC], ident[:, :])
                        ins = pe.transpose(xTp4[0:VC, j, 1, :], x1[:, q.h, j, S:FEAT], ident[:, :])
                    ins.then_inc(s["xTp"], 1)

                def turn_edges(q):
                    pe.wait_ge(s[f"ein{q.h}"], (q.u + 1) * 32 + 32 * last(q))
                    if not first(q, 1):
                        pe.wait_ge(s["h1"], q.g)
                    plain(pe)
                    for j in range(2):
                        ins = pe.transpose(hp[0:64, j * P:j * P + P], e64[:, q.h, j, :], ident[:, :])
                    ins.then_inc(s["eTp"], 1)

                def linear(q):
                    pe.wait_ge(s["xT"], q.g + 1)
                    if not first(q, 1):
                        pe.wait_ge(s["m1"], q.g)
                    for j in range(2):
                        pe.matmul(hvp[:, j, 0:S], xT[0:S, j, 0, :], k["w1s"][:, :], start=True, stop=True)
                        ins = pe.matmul(hvp[:, j, S:HW], xT[:, j, 1, :], k["w1v"][:, :], start=True, stop=True)
                    ins.then_inc(s["f"], 1)

                def network1(q):
                    pe.wait_ge(s["eT"], q.g + 1)
                    plain(pe)
                    pe.matmul(hp[0:64, 2 * P:4 * P], k["gfc1"][:, :], eT[:, :], start=True, stop=True).then_inc(s["h1p"], 1)

                def network2(q):
                    pe.wait_ge(s["h1"], q.g + 1)
                    if not first(q, 1):
                        pe.wait_ge(s["wb"], q.g)
                    for j in range(2):
                        ins = pe.matmul(wp3[:, j, :], hid[:, j * P:j * P + P], k["gfc2"][:, :], start=True, stop=True)
                    ins.then_inc(s["wp"], 1)

                def turn_mid(q):
                    pe.wait_ge(s["m1"], q.g + 1)
                    pe.wait_ge(s["m2"], q.g + 1)
                    if not first(q, 1):
                        pe.wait_ge(s["midT"], q.g)
                    for j in range(2):
                        for m in range(2):
                            ins = pe.transpose(midTp4[:, j, m, :], mid[:, j, m, :], ident[:, :])
                    ins.then_inc(s["midTp"], 1)
                    pe.wait_ge(s["m3"], q.g + 1)
                    if not first(q, 1):
                        pe.wait_ge(s["mid3T"], q.g)
                    for j in range(2):
                        ins = pe.transpose(mid3Tp[0:VC, j, :], mid3[:, j, :], ident[:, :])
                    ins.then_inc(s["mid3Tp"], 1)

                def out(q):
                    pe.wait_ge(s["midT"], q.g + 1)
                    pe.wait_ge(s["mid3T"], q.g + 1)
                    if not first(q, 1):
                        pe.wait_ge(s["msg"], q.g)
                    for j in range(2):
                        pe.matmul(msgp3[:, j, :], midT[:, j, 0, :], k["out1a"][:, :], start=True, stop=False)
                        pe.matmul(msgp3[:, j, 0:AGG1], midT[:, j, 1, :], k["out1b"][:, :], start=False, stop=False)
                        ins = pe.matmul(msgp3[:, j, 96:AGG1], mid3T[:, j, :], k["out1c"][:, :], start=False, stop=True)
                    ins.then_inc(s["msgp"], 1)

                def add_up(q):
                    pe.wait_ge(s["msg"], q.g + 1)
                    pe.wait_ge(s["eqs"], q.g + 1)
                    if not first(q, 1):
                        pe.wait_ge(s["total0"], q.g)
                    for j in range(2):
                        ins = pe.matmul(sump3[:, j, :], eq[:, j, :], msg[:, j, :], start=True, stop=True)
                    ins.then_inc(s["sump"], 1)

                passes(pe, PAIRS, [(1, linear), (2, turn_edges), (-1, add_up), (0, turn_mid), (2, network1), (2, turn),
                                   (0, out), (2, network2)])

            @block.scalar
            def _(act):
                def turned(q):
                    act.wait_ge(s["xTp"], q.g + 1)
                    if not first(q, 1):
                        act.wait_ge(s["f"], q.g)
                    act.copy(xT[:, :, :, :], xTp4[0:VC, :, :, :]).then_inc(s["xT"], 1)

                def edges_turned(q):
                    act.wait_ge(s["eTp"], q.g + 1)
                    if not first(q, 1):
                        act.wait_ge(s["h1p"], q.g)
                    act.copy(eT[:, :], hp[0:64, 0:2 * P]).then_inc(s["eT"], 1)

                def network(q):
                    act.wait_ge(s["h1p"], q.g + 1)
                    if not first(q, 1):
                        act.wait_ge(s["wp"], q.g)
                    act.activation(hid[:, :], hp[0:64, 2 * P:4 * P], ACT.Silu).then_inc(s["h1"], 1)

                def weights(q):
                    act.wait_ge(s["wp"], q.g + 1)
                    if not first(q, 1):
                        for n in ("m0", "m2", "m3"):
                            act.wait_ge(s[n], q.g)
                    act.copy(w[:, 0, :, :], wp3[:, :, 0:P]).then_inc(s["wa"], 1)

                def mid_turned(q):
                    act.wait_ge(s["midTp"], q.g + 1)
                    if not first(q, 1):
                        act.wait_ge(s["msgp"], q.g)
                    act.copy(midT[:, :, :, :], midTp4[:, :, :, :]).then_inc(s["midT"], 1)
                    act.wait_ge(s["mid3Tp"], q.g + 1)
                    act.copy(mid3T[:, :, :], mid3Tp[0:VC, :, :]).then_inc(s["mid3T"], 1)

                def scalars_out(q):
                    act.wait_ge(s["msgp"], q.g + 1)
                    if not first(q, 1):
                        act.wait_ge(s["sump"], q.g)
                    act.copy(msg[:, :, 0:96], msgp3[:, :, 0:96]).then_inc(s["msgs"], 1)

                def summed(q):
                    act.wait_ge(s["sump"], q.g + 1)
                    if not first(q, 2):
                        act.wait_ge(s[f"sc{q.h}0"], q.u * 16)
                        act.wait_ge(s[f"sc{q.h}1"], q.u * 16)
                    act.copy(total[:, q.h, :, :], sump3[:, :, :]).then_inc(s["total0"], 1)

                def equal(q):
                    if not first(q, 1):
                        act.wait_ge(s["sump"], q.g)
                    act.copy(eq[:, :, :], k["same"][:, bass.ds(q.g * 2, 2), :]).then_inc(s["eqs"], 1)

                passes(act, PAIRS, [(1, weights), (2, edges_turned), (-1, summed), (0, mid_turned), (2, network),
                                    (2, turned), (0, scalars_out), (0, equal)])

            @block.vector
            def _(dve):
                dve.tensor_tensor(a2[:, :], k["a_src"][:, :], k["a_src"][:, :], ALU.mult).then_inc(s["a2"], 1)
                dve.wait_ge(s["a2"], 1)

                def layer0(q):
                    dve.wait_ge(s[f"in{q.h}"], (q.u + 1) * 32)
                    dve.wait_ge(s[f"yin{q.h}"], (q.u + 1) * 16)
                    dve.tensor_tensor(al[:, :], agg[:, q.h, :, FEAT], a2[:, bass.ds(q.g * 2, 2)], ALU.mult).then_inc(s["al"], 1)
                    dve.wait_ge(s["al"], q.g + 1)
                    for j in range(2):
                        ins = dve.scalar_tensor_tensor(y[:, q.h, j, :], agg[:, q.h, j, 0:FEAT], al[:, j:j + 1],
                                                       yb[:, q.h, j, :], ALU.mult, ALU.add)
                    ins.then_inc(s["y"], 1)
                    dve.wait_ge(s["y"], q.g + 1)
                    for j in range(2):
                        ins = dve.bn_stats(stats[:, j, :], y[:, q.h, j, :])
                    ins.then_inc(s["st"], 1)
                    dve.wait_ge(s["st"], q.g + 1)
                    plain(dve)
                    for j in range(2):
                        ins = dve.bn_aggr(mv[:, q.h, j, :], stats[:, j, :])
                    ins.then_inc(s["mv"], 1)
                    dve.wait_ge(s["mv"], q.g + 1)
                    if not first(q, 1):
                        dve.wait_ge(s["rstd"], q.g)
                    dve.tensor_scalar(var[:, :], mv[:, q.h, :, 1], EPS, None, ALU.add).then_inc(s["var"], 1)

                def norm(q):
                    dve.wait_ge(s["rstd"], q.g + 1)
                    dve.tensor_tensor(ra[:, :], rstd[:, :], k["a_src"][:, bass.ds(q.g * 2, 2)], ALU.mult).then_inc(s["ra"], 1)
                    dve.wait_ge(s["ra"], q.g + 1)
                    if not first(q, 2):
                        dve.wait_ge(s["xTp"], q.g - 1)
                    for j in range(2):
                        ins = dve.tensor_scalar(x1[:, q.h, j, :], y[:, q.h, j, :], mv[:, q.h, j, 0:1], ra[:, j:j + 1],
                                                ALU.subtract, ALU.mult)
                    ins.then_inc(s["x1"], 1)

                def attributes(q):
                    dve.wait_ge(s[f"ein{q.h}"], (q.u + 1) * 32 + 32 * last(q))
                    dve.tensor_copy(ye[:, q.h, :, 0:3], e4[:, q.h, :, 1:4])
                    dve.tensor_copy(ye[:, q.h, :, 3:5], e4[:, q.h, :, 1:3])
                    dve.tensor_copy(ye[:, q.h, :, 5:6], e4[:, q.h, :, 0:1]).then_inc(s["ye"], 1)

                def product(q):
                    hs = hvp[:, :, 0:S].unsqueeze(2).to_broadcast([P, 2, 2, S])
                    hv = hvp[:, :, S:HW].rearrange("p j (c u) -> p j c u", c=5)
                    yc = [ye[:, q.h, :, c:c + 3].unsqueeze(3).to_broadcast([P, 2, C, V]) for c in range(3)]
                    y0 = ye[:, q.h, :, 5:6].to_broadcast([P, 2, 96])
                    dve.wait_ge(s["ye"], q.g + 1)
                    dve.wait_ge(s["f"], q.g + 1)
                    dve.tensor_tensor(ca[:, :, :, :], hv[:, :, 1:4, :], yc[2], ALU.mult)
                    dve.tensor_tensor(cb[:, :, :, :], hv[:, :, 2:5, :], yc[1], ALU.mult).then_inc(s["ca"], 1)
                    dve.tensor_tensor(dot[:, :, :, :], hv[:, :, 0:3, :], yc[0], ALU.mult).then_inc(s["dot"], 1)
                    dve.wait_ge(s["ca"], q.g + 1)
                    dve.tensor_tensor(cc[:, :, :, :], ca[:, :, :, :], cb[:, :, :, :], ALU.subtract).then_inc(s["cc"], 1)
                    dve.wait_ge(s["dot"], q.g + 1)
                    dve.tensor_reduce(dots[:, :, :], dot[:, :, :, :].rearrange("p j c u -> p j u c"), AX.X,
                                      ALU.add).then_inc(s["dots"], 1)
                    dve.wait_ge(s["wa"], q.g + 1)
                    dve.tensor_tensor(w[:, 1, :, 0:96], wp3[:, :, P:W1N], y0, ALU.mult).then_inc(s["wb"], 1)
                    dve.wait_ge(s["cc"], q.g + 1)
                    if not first(q, 1):
                        dve.wait_ge(s["midTp"], q.g)
                        dve.wait_ge(s["mid3Tp"], q.g)
                    dve.tensor_tensor(mid3[:, :, :].rearrange("p j (c u) -> p j c u", c=C), cc[:, :, :, :],
                                      w[:, 0, :, 96:P].unsqueeze(2).to_broadcast([P, 2, C, V]), ALU.mult).then_inc(s["m3"], 1)
                    dve.wait_ge(s["dots"], q.g + 1)
                    dve.tensor_tensor(mid[:, :, 1, VC:P], dots[:, :, :], w[:, 0, :, 64:96], ALU.mult).then_inc(s["m2"], 1)
                    dve.wait_ge(s["wb"], q.g + 1)
                    dve.tensor_tensor(mid[:, :, 0, :].rearrange("p j (m n) -> p j m n", m=2),
                                      w[:, :, :, 0:S].rearrange("p m j n -> p j m n"), hs, ALU.mult).then_inc(s["m0"], 1)
                    dve.tensor_tensor(mid[:, :, 1, 0:VC].rearrange("p j (c u) -> p j c u", c=C), hv[:, :, 0:3, :],
                                      w[:, 1, :, 64:96].unsqueeze(2).to_broadcast([P, 2, C, V]), ALU.mult).then_inc(s["m1"], 1)

                def vectors_out(q):
                    dve.wait_ge(s["msgs"], q.g + 1)
                    y1 = ye[:, q.h, :, 0:3].unsqueeze(3).to_broadcast([P, 2, C, V])
                    qv = msgp3[:, :, AGG1:MSG1].unsqueeze(2).to_broadcast([P, 2, C, V])
                    dve.tensor_tensor(qy[:, :, :, :], qv, y1, ALU.mult).then_inc(s["qy"], 1)
                    dve.wait_ge(s["qy"], q.g + 1)
                    if not first(q, 1):
                        dve.wait_ge(s["sump"], q.g)
                    dve.tensor_tensor(msg[:, :, 96:AGG1].rearrange("p j (u c) -> p j c u", c=C), qy[:, :, :, :],
                                      msgp3[:, :, 96:AGG1].rearrange("p j (c u) -> p j c u", c=C),
                                      ALU.add).then_inc(s["msg"], 1)

                passes(dve, PAIRS, [(2, norm), (1, attributes), (1, product), (3, layer0), (0, vectors_out)])
                dve.drain()


def nodes(nc, t, k, bank, wide, other):
    ctx, sb, sem = phase(nc)
    with ctx:
        x = sb("n_x", [P, 2, J, FEAT])
        s0 = sb("n_s0", [P, 2, J, AGG0])
        s1 = sb("n_s1", [P, 2, J, AGG1])
        a = sb("n_a", [P, NGROUPS, J])
        half = sb("n_half", [P, J])
        xsT = sb("n_xsT", [S, J * P])
        xvT = sb("n_xvT", [VC, J * P])
        al = sb("n_al", [P, J])
        al2 = sb("n_al2", [P, J])
        b = sb("n_b", [P, 2, J, FEAT])
        y = sb("n_y", [P, 2, J, FEAT])
        stats = sb("n_stats", [P, J, 6])
        mv = sb("n_mv", [P, 2, J, 2])
        var = sb("n_var", [P, J])
        rstd = sb("n_rstd", [P, 2, J])
        shift = sb("n_shift", [P, 2, J])
        x1 = sb("n_x1", [P, 2, J, FEAT])
        x1sT = sb("n_x1sT", [S, J * P])
        x1vT = sb("n_x1vT", [VC, J * P])
        gate = sb("n_gate", [P, J, 96])
        m = sb("n_m", [P, J, FEAT])
        z = sb("n_z", [P, 2, J, FEAT])
        stats1 = sb("n_stats1", [P, J, 6])
        mv1 = sb("n_mv1", [P, 2, J, 2])
        var1 = sb("n_var1", [P, J])
        rstd1 = sb("n_rstd1", [P, 2, J])
        shift1 = sb("n_shift1", [P, 2, J])
        res = sb("n_res", [P, 2, J, FEAT])
        names = ("passed half a in0 in1 s1in0 s1in1 xT xTc sc al al2 b0 b y st mv var rstd shift x1 x1T x1Tc pre gate ms m z "
                 "st1 mv1 var1 rstd1 shift1 ra rp out0 out1").split()
        s = {n: sem("n_" + n) for n in names}
        scp = wide[:, :, 0:2 * FEAT].rearrange("p b (i c) -> p b i c", i=2)
        prep = other[:, :, 0:2 * AGG1].rearrange("p b (i c) -> p b i c", i=2)

        def first(q, n):
            return isinstance(q.g, int) and q.g < n

        def last(q):
            return isinstance(q.g, int) and q.g == NGROUPS - 1

        def part(name, q):
            v = t[name][NODES - J * P:NODES, :] if last(q) else t[name][bass.ds(q.g * (J * P), J * P), :]
            return v.rearrange("(p j) c -> p (j c)", j=J)

        def rows(v):
            return v.rearrange("p j c -> p (j c)")

        def four(v):
            return v.rearrange("p (b i) c -> p b i c", b=2)

        def av(q):
            return a[:, bass.ds(q.g, 1), :].rearrange("p g j -> p (g j)")

        def a1(q, j):
            return a[:, bass.ds(q.g, 1), j:j + 1].rearrange("p g j -> p (g j)")

        def plain(engine):
            engine.sem_inc(s["passed"], 1)

        with nc.Block() as block:

            @block.sync
            def _(sp):
                whole = (NGROUPS - 1) * J * P
                sp.dma_start(a[:, 0:NGROUPS - 1, :],
                             t["node_vec1"][0:whole, :].rearrange("(g p j) c -> p g (j c)", p=P, j=J)).then_inc(s["a"], 16)
                sp.dma_start(a[:, NGROUPS - 1, :],
                             t["node_vec1"][NODES - J * P:NODES, :].rearrange("(p j) c -> p (j c)", j=J)).then_inc(s["a"], 16)

                def load(q):
                    if not first(q, 2):
                        sp.wait_ge(s["xT"], q.g - 1)
                        sp.wait_ge(s["b"], q.g - 1)
                    sp.dma_start(rows(x[:, q.h, :, :]), part("x", q)).then_inc(s[f"in{q.h}"], 16)
                    sp.dma_start(rows(s0[:, q.h, :, :]), part("agg0", q)).then_inc(s[f"in{q.h}"], 16)

                def load1(q):
                    if not first(q, 2):
                        sp.wait_ge(s["pre"], q.g - 1)
                    sp.dma_start(rows(s1[:, q.h, :, :]), part("agg1", q)).then_inc(s[f"s1in{q.h}"], 16)

                def store(q):
                    sp.wait_ge(s["ra"], q.g + 1)
                    sp.wait_ge(s["rp"], q.g + 1)
                    if last(q):
                        sp.wait_ge(s[f"out{1 - q.h}"], (q.u + q.h) * 16)
                    sp.dma_start(part("out", q), rows(res[:, q.h, :, :])).then_inc(s[f"out{q.h}"], 16)

                passes(sp, NGROUPS, [(4, load), (1, load1), (-1, store)])
                for n in ("out0", "out1"):
                    sp.wait_ge(s[n], 16 * (NGROUPS // 2))

            @block.gpsimd
            def _(pool):
                pool.memset(half[:, :], -0.5).then_inc(s["half"], 1)
                pool.wait_ge(s["half"], 1)
                pool.wait_ge(s["a"], 32)

                def root(v, r, vs, rs, free):
                    def of(q):
                        pool.wait_ge(s[vs], q.g + 1)
                        if not first(q, 2):
                            pool.wait_ge(s[free], q.g - 1)
                        pool.tensor_tensor(r[:, q.h, :], v[:, :], half[:, :], ALU.pow).then_inc(s[rs], 1)
                    return of

                def sums0(q):
                    pool.wait_ge(s[f"in{q.h}"], (q.u + 1) * 32)
                    plain(pool)
                    pool.tensor_tensor(al[:, :], s0[:, q.h, :, FEAT], av(q), ALU.mult).then_inc(s["al"], 1)
                    pool.wait_ge(s["al"], q.g + 1)
                    plain(pool)
                    pool.tensor_tensor(al2[:, :], al[:, :], av(q), ALU.mult).then_inc(s["al2"], 1)
                    pool.wait_ge(s["al2"], q.g + 1)
                    if not first(q, 2):
                        pool.wait_ge(s["y"], q.g - 1)
                    pool.tensor_tensor(b[:, q.h, :, :], s0[:, q.h, :, 0:FEAT],
                                       al2[:, :].unsqueeze(2).to_broadcast([P, J, FEAT]), ALU.mult).then_inc(s["b0"], 1)
                    pool.wait_ge(s["b0"], q.g + 1)
                    pool.tensor_tensor(b[:, q.h, :, :], b[:, q.h, :, :], x[:, q.h, :, :], ALU.add).then_inc(s["b"], 1)

                def norm1(q):
                    pool.wait_ge(s["shift1"], q.g + 1)
                    if not first(q, 2):
                        pool.wait_ge(s[f"out{q.h}"], q.u * 16)
                    plain(pool)
                    for j in range(NACT, J):
                        ins = pool.tensor_scalar(res[:, q.h, j, :], z[:, q.h, j, :], rstd1[:, q.h, j:j + 1],
                                                 shift1[:, q.h, j:j + 1], ALU.mult, ALU.add)
                    ins.then_inc(s["rp"], 1)

                passes(pool, NGROUPS, [(-1, root(var1, rstd1, "var1", "rstd1", "ra")),
                                       (2, root(var, rstd, "var", "rstd", "x1")), (-1, norm1), (3, sums0)])

            @block.tensor
            def _(pe):
                ident = k["ident"]

                def product1(q):
                    pe.wait_ge(s["x1Tc"], q.g + 1)
                    pe.wait_ge(s[f"s1in{q.h}"], (q.u + 1) * 16)
                    if not first(q, 1):
                        pe.wait_ge(s["m"], q.g)
                    for j in range(J):
                        o = prep[:, j // 2, j % 2, :]
                        pe.matmul(o, ident[:, :], s1[:, q.h, j, :], start=True, stop=False)
                        pe.matmul(o[:, 0:96], x1sT[:, j * P:j * P + P], k["sc1s"][:, :], start=False, stop=False)
                        ins = pe.matmul(o[:, 96:AGG1], x1vT[:, j * P:j * P + P], k["sc1v"][:, :], start=False, stop=True)
                    ins.then_inc(s["pre"], 1)

                def turn(src, banks, ready, free, done):
                    def of(q):
                        pe.wait_ge(*ready(q))
                        if not first(q, 1):
                            pe.wait_ge(s[free], q.g)
                        plain(pe)
                        for j in range(J):
                            pe.transpose(banks[0][0:S, j * P:j * P + P], src[:, q.h, j, 0:S], ident[:, :])
                            ins = pe.transpose(banks[1][0:VC, j * P:j * P + P], src[:, q.h, j, S:FEAT], ident[:, :])
                        ins.then_inc(s[done], 1)
                    return of

                def product0(q):
                    pe.wait_ge(s["xTc"], q.g + 1)
                    if not first(q, 1):
                        pe.wait_ge(s["y"], q.g)
                    for j in range(J):
                        o = scp[:, j // 2, j % 2, :]
                        pe.matmul(o[:, 0:S], xsT[:, j * P:j * P + P], k["w0s"][:, S:2 * S], start=True, stop=True)
                        ins = pe.matmul(o[:, S:FEAT], xvT[:, j * P:j * P + P], k["w0v"][:, 0:VC], start=True, stop=True)
                    ins.then_inc(s["sc"], 1)

                passes(pe, NGROUPS, [
                    (0, product1),
                    (3, turn(x, bank[0:2], lambda q: (s[f"in{q.h}"], (q.u + 1) * 32), "xTc", "xT")),
                    (1, turn(x1, bank[2:4], lambda q: (s["x1"], q.g + 1), "x1Tc", "x1T")),
                    (3, product0)])

            @block.scalar
            def _(act):
                act.wait_ge(s["a"], 32)

                def gates(q):
                    act.wait_ge(s["pre"], q.g + 1)
                    if not first(q, 1):
                        act.wait_ge(s["m"], q.g)
                    for j in range(J):
                        ins = act.activation(gate[:, j, :], prep[:, j // 2, j % 2, 0:96], ACT.Sigmoid, scale=a1(q, j))
                    ins.then_inc(s["gate"], 1)

                def turned(banks, to, ready, free, done):
                    def of(q):
                        act.wait_ge(s[ready], q.g + 1)
                        if not first(q, 1):
                            act.wait_ge(s[free], q.g)
                        act.copy(to[0][:, :], banks[0][0:S, :])
                        act.copy(to[1][:, :], banks[1][0:VC, :]).then_inc(s[done], 1)
                    return of

                def norm0(q):
                    act.wait_ge(s["shift"], q.g + 1)
                    if not first(q, 2):
                        act.wait_ge(s["z"], q.g - 1)
                        act.wait_ge(s["x1T"], q.g - 1)
                    for j in range(J):
                        ins = act.activation(x1[:, q.h, j, :], y[:, q.h, j, :], ACT.Identity, bias=shift[:, q.h, j:j + 1],
                                             scale=rstd[:, q.h, j:j + 1])
                    ins.then_inc(s["x1"], 1)

                def norm1(q):
                    act.wait_ge(s["shift1"], q.g + 1)
                    if not first(q, 2):
                        act.wait_ge(s[f"out{q.h}"], q.u * 16)
                    for j in range(NACT):
                        ins = act.activation(res[:, q.h, j, :], z[:, q.h, j, :], ACT.Identity,
                                             bias=shift1[:, q.h, j:j + 1], scale=rstd1[:, q.h, j:j + 1])
                    ins.then_inc(s["ra"], 1)

                passes(act, NGROUPS, [(1, norm0), (-1, norm1), (0, gates),
                                      (3, turned(bank[0:2], (xsT, xvT), "xT", "sc", "xTc")),
                                      (1, turned(bank[2:4], (x1sT, x1vT), "x1T", "pre", "x1Tc"))])

            @block.vector
            def _(dve):
                dve.wait_ge(s["a"], 32)

                def moments(q, of, st, mv_, v, ready, n, var_free):
                    dve.wait_ge(s[ready], q.g + 1)
                    for j in range(J):
                        ins = dve.bn_stats(st[:, j, :], of[:, q.h, j, :])
                    ins.then_inc(s["st" + n], 1)
                    dve.wait_ge(s["st" + n], q.g + 1)
                    plain(dve)
                    for j in range(J):
                        ins = dve.bn_aggr(mv_[:, q.h, j, :], st[:, j, :])
                    ins.then_inc(s["mv" + n], 1)
                    dve.wait_ge(s["mv" + n], q.g + 1)
                    if not first(q, 1):
                        dve.wait_ge(s[var_free], q.g)
                    dve.tensor_scalar(v[:, :], mv_[:, q.h, :, 1], EPS, None, ALU.add).then_inc(s["var" + n], 1)

                def layer0(q):
                    dve.wait_ge(s["sc"], q.g + 1)
                    dve.wait_ge(s["b"], q.g + 1)
                    if not first(q, 2):
                        dve.wait_ge(s["x1"], q.g - 1)
                    for j in range(J):
                        ins = dve.scalar_tensor_tensor(y[:, q.h, j, :], scp[:, j // 2, j % 2, :], a1(q, j), b[:, q.h, j, :],
                                                       ALU.mult, ALU.add)
                    ins.then_inc(s["y"], 1)
                    moments(q, y, stats, mv, var, "y", "", "rstd")

                def layer1(q):
                    dve.wait_ge(s["gate"], q.g + 1)
                    dve.tensor_tensor(four(m[:, :, 0:S]), prep[:, :, :, 0:S], four(gate[:, :, 0:S]), ALU.mult).then_inc(s["ms"], 1)
                    for d in range(2):
                        ins = dve.tensor_tensor(
                            m[:, 2 * d:2 * d + 2, S:FEAT].rearrange("p j (u c) -> p j u c", c=C),
                            prep[:, d, :, 96:AGG1].rearrange("p j (u c) -> p j u c", c=C),
                            gate[:, 2 * d:2 * d + 2, S:96].unsqueeze(3).to_broadcast([P, 2, V, C]), ALU.mult)
                    ins.then_inc(s["m"], 1)
                    dve.wait_ge(s["m"], q.g + 1)
                    if not first(q, 2):
                        dve.wait_ge(s["ra"], q.g - 1)
                        dve.wait_ge(s["rp"], q.g - 1)
                    for j in range(J):
                        ins = dve.scalar_tensor_tensor(z[:, q.h, j, :], m[:, j, :], a1(q, j), x1[:, q.h, j, :],
                                                       ALU.mult, ALU.add)
                    ins.then_inc(s["z"], 1)
                    moments(q, z, stats1, mv1, var1, "z", "1", "rstd1")

                def shifts(mv_, r, to, rs, done):
                    def of(q):
                        dve.wait_ge(s[rs], q.g + 1)
                        dve.scalar_tensor_tensor(to[:, q.h, :], mv_[:, q.h, :, 0], -1.0, r[:, q.h, :], ALU.mult,
                                                 ALU.mult).then_inc(s[done], 1)
                    return of

                passes(dve, NGROUPS, [(2, layer0), (-1, shifts(mv1, rstd1, shift1, "rstd1", "shift1")), (0, layer1),
                                      (2, shifts(mv, rstd, shift, "rstd", "shift"))])
                dve.drain()


SCRATCH = {"agg0": (TABLE, AGG0), "agg1": (TABLE, AGG1), "ybase": (PAIRS, P, 2, FEAT)}


def kernel(**inputs):
    import numpy as _np
    import concourse.bacc as _bacc
    from concourse.bass_utils import run_bass_kernel_spmd as _run

    nc = _bacc.Bacc("TRN2", target_bir_lowering=False, num_devices=1)
    arrays, t = {}, {}
    for name, given in inputs.items():
        a = _np.ascontiguousarray(given)
        arrays[f"in_{name}"] = a
        t[name] = nc.dram_tensor(f"in_{name}", a.shape, mybir.dt.from_np(a.dtype), kind="ExternalInput").ap()
    for name, shape in SCRATCH.items():
        t[name] = nc.dram_tensor(f"d_{name}", list(shape), F32, kind="Internal").ap()
    t["out"] = nc.dram_tensor("out", [NODES, FEAT], F32, kind="ExternalOutput").ap()
    build(nc, t)
    r = _run(nc, [arrays], core_ids=[0])
    return r.results[0]["out"]
```

```python
from contextlib import ExitStack

import concourse.bass as bass
from concourse import mybir

F32 = mybir.dt.float32
BF16 = mybir.dt.bfloat16
I32 = mybir.dt.int32
ALU = mybir.AluOpType
ACT = mybir.ActivationFunctionType
AX = mybir.AxisListType

P = 128
NODES, FEAT = 100000, 160
EDGES = 25000
S, V, C = 64, 32, 3
VC = V * C
TILES = -(-EDGES // P)
TAIL = EDGES - (TILES - 1) * P
PAIRS = TILES // 2
ROWS = 784
TABLE = P * ROWS
SPARE = NODES + 1
ZROWS = 8
NZ = ROWS // ZROWS
AGG0 = FEAT + 1
AGG1 = 96 + VC
MSG0 = AGG0 + V
MSG1 = AGG1 + V
W0N, W1N = 192, 224
AT = 7
J = 4
NGROUPS = -(-NODES // (J * P))
NACT = 2
EPS = 1e-5
assert TILES % (2 * AT) == 0 and SPARE + P <= TABLE and NGROUPS % 2 == 0 and ROWS % ZROWS == 0


class Group:

    def __init__(self, g, h, u):
        self.g, self.h, self.u = g, h, u


UNROLL = 6


def passes(engine, count, stages):
    leads = [lead for lead, _ in stages]
    lo, hi = 2 - min(leads), count - 1 - max(leads)
    n = (hi - lo) // UNROLL

    def peeled(p):
        for lead, stage in stages:
            if 0 <= p + lead < count:
                stage(Group(p + lead, (p + lead) % 2, (p + lead) // 2))

    for p in range(-max(leads), lo):
        peeled(p)
    with engine.Fori(0, n) as i:
        for k in range(UNROLL):
            for lead, stage in stages:
                c = lo + k + lead
                stage(Group(i * UNROLL + c, c % 2, i * (UNROLL // 2) + c // 2))
    for p in range(lo + UNROLL * n, count - min(leads)):
        peeled(p)


def build(nc, t):
    with ExitStack() as whole:
        k = {}

        def keep(name, shape, dt=F32):
            k[name] = whole.enter_context(nc.sbuf_tensor(name, shape, dt))
            return k[name]

        bank = [whole.enter_context(nc.psum_tensor(f"bank{b}", [P, 512], F32)) for b in range(4)]
        pairs = [whole.enter_context(nc.psum_tensor(f"pair{b}", [P, 2, 512], F32)) for b in range(2)]
        wide, other = pairs
        bank += [other[:, 0, :], other[:, 1, :]]
        keep("ident", [P, P])
        keep("same", [P, TILES, P], BF16)
        keep("src", [P, TILES], I32)
        keep("row", [P, TILES], I32)
        keep("a_src", [P, TILES])
        keep("w0s", [P, 2 * S])
        keep("w0v", [P, 2 * VC])
        keep("fc1", [2 * 8, P])
        keep("fc2", [P, P])
        keep("fc3", [P, 2 * W0N])
        keep("out0a", [P, MSG0])
        keep("out0b", [P, AGG0])
        keep("w1s", [P, S])
        keep("w1v", [P, 5 * V])
        keep("gfc1", [P, P])
        keep("gfc2", [P, 2 * W1N])
        keep("out1a", [P, MSG1])
        keep("out1b", [P, AGG1])
        keep("out1c", [VC, VC])
        keep("sc1s", [P, 96])
        keep("sc1v", [P, VC])
        prepare(nc, t, k, bank, wide)
        edges0(nc, t, k, bank, wide)
        if t.get("stop") == 0:
            return
        edges1(nc, t, k, bank, wide)
        if t.get("stop") == 1:
            return
        nodes(nc, t, k, bank, wide, other)


def phase(nc):
    ctx = ExitStack()
    sb = lambda name, shape, dt=F32: ctx.enter_context(nc.sbuf_tensor(name, shape, dt))
    sem = lambda name: ctx.enter_context(nc.semaphore(name))
    return ctx, sb, sem


def prepare(nc, t, k, bank, wide):
    ctx, sb, sem = phase(nc)
    with ctx:
        zero = sb("zero", [P, ZROWS * AGG0])
        tri = sb("tri", [P, P])
        count_i = sb("count_i", [P, 1], I32)
        own = sb("own", [P, 1])
        stage = sb("stage", [P, 1700])
        ids = sb("ids", [P, 4, P], I32)
        idf = sb("idf", [P, 4, P])
        srcf = sb("srcf", [P, TILES])
        dstf = sb("dstf", [P, TILES])
        spread = sb("spread", [P, 2, 2, P])
        of = sb("of", [P, C])
        below = sb("below", [P, 2, P])
        idx = sb("a_idx", [P, 2, AT], I32)
        got = sb("a_got", [P, 2, AT])
        earlier = sb("earlier", [P, TILES])
        s_zero, s_zeroed = sem("s_zero"), [sem("s_zeroed0"), sem("s_zeroed1")]
        s_staged, s_in, s_ids, s_const = sem("s_staged"), sem("s_in"), sem("s_ids"), sem("s_const")
        s_idf, s_turned, s_ids_up = sem("s_idf"), sem("s_turned"), sem("s_ids_up")
        s_src, s_idx, s_kept, s_passed = sem("s_src"), sem("s_idx"), sem("s_kept"), sem("s_passed")
        s_got = [sem("s_got0"), sem("s_got1")]
        s_spread, s_rows, s_same, s_below, s_red, s_dve = (
            sem("s_spread"), sem("s_rows"), sem("s_same"), sem("s_below"), sem("s_red"), sem("s_dve"))
        half = TILES // 2
        parts = [("src", 0), ("dst", 2)]
        loads = []

        def load(name, r0, r1, p0, c0):
            cols = t[name].shape[1]
            loads.append((stage[p0:p0 + r1 - r0, c0:c0 + cols], t[name][r0:r1, :]))
            return stage[p0:p0 + r1 - r0, c0:c0 + cols]

        c = [0]

        def at(width):
            c[0] += width
            return c[0] - width

        def thrice(name, r0=0):
            a = at(t[name].shape[1])
            return [load(name, r0, r0 + V, V * i, a) for i in range(C)]

        def woven(name):
            a = at(V)
            for i in range(C):
                loads.append((stage[V + i:P:C, a:a + V], t[name][:, :]))
            return stage[:, a:a + V]

        def diagonal(name):
            n, m = t[name].shape
            a = at(2 * m)
            for j in range(2):
                load(name, 0, n, j * n, a + j * m)
            return stage[0:2 * n, a:a + 2 * m]

        def twice(name):
            a = at(t[name].shape[1])
            return [load(name, 0, 64, 64 * j, a) for j in range(2)]

        wl10, wsc0 = load("L0_gnn_Wl1_0", 0, S, 0, at(64)), load("L0_gnn_Wsc0", 0, S, 0, at(64))
        wl11, wsc1 = woven("L0_gnn_Wl1_1"), woven("L0_gnn_Wsc1")
        wfc1, wfc2 = diagonal("L0_gnn_Wfc1"), diagonal("L0_gnn_Wfc2")
        wfc3 = twice("L0_gnn_Wfc3")
        x = at(64)
        l2s_a, l2s_b = load("L0_gnn_Wl2_s", 0, 64, 64, x), load("L0_gnn_Wl2_s", 64, 96, 96, at(64))
        x = at(1)
        wa_a, wa_b = load("L0_gnn_Wa", 0, 64, 64, x), load("L0_gnn_Wa", 64, 96, 96, at(1))
        l2v_a, l2v_b = load("L0_gnn_Wl2_v", 0, 64, 0, at(32)), thrice("L0_gnn_Wl2_v", 64)
        gws, gwv = load("L1_gnn_lin1_ws", 0, S, 0, at(64)), woven("L1_gnn_lin1_wv")
        gf1, gf2 = diagonal("L1_gnn_fc_w1"), twice("L1_gnn_fc_w2")
        x = at(96)
        m2s_a, m2s_b = load("L1_gnn_lin2_ws", 0, 64, 64, x), load("L1_gnn_lin2_ws", 64, 96, 96, at(96))
        m2v_a = load("L1_gnn_lin2_wv", 0, 64, 0, at(32))
        m2v_b, m2v_c = thrice("L1_gnn_lin2_wv", 64), thrice("L1_gnn_lin2_wv", 96)
        gscs, gscv = load("L1_gnn_sc_ws", 0, S, 0, at(96)), woven("L1_gnn_sc_wv")
        assert c[0] <= 1700
        n_in = 16 * len(loads)

        with nc.Block() as block:

            @block.sync
            def _(sp):
                for name, at_ in parts:
                    full = t[name][0:(TILES - 1) * P].rearrange("(t p) -> t p", p=P)
                    if at_ == 0:
                        sp.wait_ge(s_ids, 1)
                    sp.dma_start(ids[0:half, at_, :], full[0:half, :]).then_inc(s_ids_up, 16)
                    sp.dma_start(ids[0:half - 1, at_ + 1, :], full[half:2 * half - 1, :]).then_inc(s_ids_up, 16)
                    sp.dma_start(ids[half - 1:half, at_ + 1, 0:TAIL],
                                 t[name][(TILES - 1) * P:EDGES].rearrange("(t p) -> t p", t=1)).then_inc(s_ids_up, 16)
                sp.wait_ge(s_staged, 1)
                for dst, src in loads:
                    sp.dma_start(dst, src).then_inc(s_in, 16)
                table = t["agg0"].rearrange("(p r) c -> p (r c)", p=P)
                sp.wait_ge(s_zero, 1)

                def clear(q):
                    if not (isinstance(q.g, int) and q.g < 2):
                        sp.wait_ge(s_zeroed[q.h], q.u * 16)
                        sp.sem_inc(s_passed, 1)
                    sp.dma_start(table[:, bass.ds(q.g * (ZROWS * AGG0), ZROWS * AGG0)], zero[:, :]).then_inc(s_zeroed[q.h], 16)

                passes(sp, NZ, [(0, clear)])
                for h in range(2):
                    sp.wait_ge(s_zeroed[h], 16 * (NZ // 2))

            @block.gpsimd
            def _(pool):
                pool.memset(ids[:, 0:2, :], 0)
                pool.memset(ids[:, 2:4, :], NODES).then_inc(s_ids, 1)
                pool.memset(stage[:, :], 0.0).then_inc(s_staged, 1)
                pool.memset(zero[:, :], 0.0).then_inc(s_zero, 1)
                pool.memset(k["ident"][:, :], 1.0)
                pool.memset(tri[:, :], 1.0).then_inc(s_const, 1)
                pool.wait_ge(s_const, 1)
                pool.affine_select(out=k["ident"][:, :], in_=k["ident"][:, :], compare_op=ALU.is_equal, fill=0.0,
                                   base=0, pattern=[[-1, P]], channel_multiplier=1).then_inc(s_const, 1)
                pool.affine_select(out=tri[:, :], in_=tri[:, :], compare_op=ALU.is_gt, fill=0.0, base=0,
                                   pattern=[[-1, P]], channel_multiplier=1).then_inc(s_const, 1)
                pool.iota(count_i[:, :], pattern=[[0, 1]], base=SPARE, channel_multiplier=1).then_inc(s_const, 1)

                def gather(q):
                    pool.tensor_copy(idx[:, q.h, :], k["src"][:, bass.ds(q.g * AT, AT)]).then_inc(s_idx, 1)
                    pool.wait_ge(s_idx, q.g + 1)
                    if not (isinstance(q.g, int) and q.g < 2):
                        pool.wait_ge(s_kept, q.g - 1)
                    pool.sem_inc(s_passed, 1)
                    for j in range(AT):
                        at = bass.IndirectOffsetOnAxis(ap=idx[:, q.h, j:j + 1], axis=0)
                        pool.indirect_dma_start(got[:, q.h, j:j + 1], None, t["node_vec1"], at).then_inc(s_got[q.h], 16)

                def keep(q):
                    pool.wait_ge(s_got[q.h], (q.u + 1) * 16 * AT)
                    pool.tensor_copy(k["a_src"][:, bass.ds(q.g * AT, AT)], got[:, q.h, :]).then_inc(s_kept, 1)

                pool.wait_ge(s_src, 1)
                passes(pool, TILES // AT, [(1, gather), (0, keep)])

            @block.tensor
            def _(pe):
                pe.wait_ge(s_const, 3)
                pe.wait_ge(s_idf, 1)
                for j in range(4):
                    ins = pe.transpose(bank[0][:, j * P:j * P + half], idf[0:half, j, :], k["ident"][0:half, 0:half])
                ins.then_inc(s_turned, 1)

                def turn(q):
                    pe.wait_ge(s_spread, q.g + 1)
                    if not (isinstance(q.g, int) and q.g < 1):
                        pe.wait_ge(s_same, q.g)
                    for j in range(2):
                        ins = pe.transpose(bank[1][:, j * P:j * P + P], spread[:, q.h, j, :], k["ident"][:, :])
                    ins.then_inc(s_rows, 1)

                passes(pe, PAIRS, [(0, turn)])

            @block.scalar
            def _(act):
                def spread_dst(q):
                    if not (isinstance(q.g, int) and q.g < 2):
                        act.wait_ge(s_rows, q.g - 1)
                    v = dstf[:, bass.ds(q.g * 2, 2)].unsqueeze(2).to_broadcast([P, 2, P])
                    act.copy(spread[:, q.h, :, :], v).then_inc(s_spread, 1)

                act.wait_ge(s_turned, 2)
                passes(act, PAIRS, [(1, spread_dst)])

            @block.vector
            def _(dve):
                done = [0]

                def link(ins):
                    done[0] += 1
                    ins.then_inc(s_dve, 1)
                    dve.wait_ge(s_dve, done[0])

                def scaled(out, in_, scale):
                    return dve.tensor_scalar(out, in_, float(scale), None, ALU.mult)

                dve.wait_ge(s_ids_up, 96)
                dve.tensor_copy(idf[:, :, :], ids[:, :, :]).then_inc(s_idf, 1)
                dve.wait_ge(s_const, 4)
                dve.tensor_copy(own[:, :], count_i[:, :])
                for name in ("w0s", "fc3", "out0a", "out0b", "w1s", "gfc2", "out1a", "out1b", "out1c", "sc1s"):
                    dve.memset(k[name][:, :], 0.0)
                dve.wait_ge(s_turned, 1)
                for m, to in ((0, srcf), (2, dstf)):
                    for j in range(2):
                        ins = dve.tensor_copy(to[:, j * half:(j + 1) * half], bank[0][:, (m + j) * P:(m + j) * P + half])
                link(ins)
                dve.sem_inc(s_turned, 1)
                dve.tensor_copy(k["src"][:, :], srcf[:, :]).then_inc(s_src, 1)

                def compare(q):
                    dve.wait_ge(s_rows, q.g + 1)
                    for j in range(2):
                        ins = dve.tensor_scalar(k["same"][:, bass.ds(q.g * 2 + j, 1), :].rearrange("p a b -> p (a b)"), bank[1][:, j * P:j * P + P],
                                                dstf[:, bass.ds(q.g * 2 + j, 1)], None, ALU.is_equal)
                    ins.then_inc(s_same, 1)
                    dve.wait_ge(s_same, q.g + 1)
                    tri2 = tri[:, :].unsqueeze(1).to_broadcast([P, 2, P])
                    dve.tensor_tensor(below[:, :, :], k["same"][:, bass.ds(q.g * 2, 2), :], tri2,
                                      ALU.mult).then_inc(s_below, 1)

                def count(q):
                    dve.wait_ge(s_below, q.g + 1)
                    dve.tensor_reduce(earlier[:, bass.ds(q.g * 2, 2)], below[:, :, :], AX.X, ALU.add).then_inc(s_red, 1)

                dve.wait_ge(s_const, 3)
                passes(dve, PAIRS, [(-1, count), (0, compare)])
                dve.wait_ge(s_red, PAIRS)

                link(dve.tensor_scalar(earlier[:, :], earlier[:, :], 0.0, None, ALU.is_gt))
                link(dve.tensor_scalar(srcf[:, :], dstf[:, :], -1.0, own[:, 0:1], ALU.mult, ALU.add))
                link(dve.tensor_tensor(srcf[:, :], srcf[:, :], earlier[:, :], ALU.mult))
                link(dve.tensor_tensor(dstf[:, :], dstf[:, :], srcf[:, :], ALU.add))
                link(dve.tensor_copy(k["row"][:, :], dstf[:, :]))

                dve.wait_ge(s_in, n_in)
                scaled(k["w0s"][0:S, 0:S], wl10, 1 / 8)
                scaled(k["w0s"][0:S, S:2 * S], wsc0, 1 / 8)
                scaled(k["fc1"][:, :], wfc1, 8 ** -0.5)
                scaled(k["fc2"][:, :], wfc2, 1 / 8)
                for j in range(2):
                    for to, c0, n in ((0, 64, 64), (64, 160, 32), (96, 0, 64), (160, 128, 32)):
                        scaled(k["fc3"][64 * j:64 * j + 64, W0N * j + to:W0N * j + to + n], wfc3[j][:, c0:c0 + n], 1 / 8)
                n0 = 32 ** -0.5 * 96 ** -0.5
                scaled(k["out0a"][0:64, AGG0:MSG0], l2v_a, n0)
                scaled(k["out0a"][64:128, 0:64], l2s_a, n0)
                scaled(k["out0a"][64:128, 64:65], wa_a, n0)
                scaled(k["out0b"][96:128, 0:64], l2s_b, n0 * 3 ** -0.5)
                scaled(k["out0b"][96:128, 64:65], wa_b, n0 * 3 ** -0.5)
                scaled(k["w1s"][0:S, :], gws, 1 / 8)
                scaled(k["gfc1"][:, :], gf1, 1 / 8)
                for j in range(2):
                    for to, c0, n in ((0, 64, 64), (64, 160, 32), (96, 192, 32), (128, 0, 64), (192, 128, 32)):
                        scaled(k["gfc2"][64 * j:64 * j + 64, W1N * j + to:W1N * j + to + n], gf2[j][:, c0:c0 + n], 1 / 8)
                n1s, n1v = 0.25 * 96 ** -0.5, 0.25 * 128 ** -0.5
                scaled(k["out1a"][0:64, AGG1:MSG1], m2v_a, n1v)
                scaled(k["out1a"][64:128, 0:96], m2s_a, n1s)
                scaled(k["out1b"][96:128, 0:96], m2s_b, n1s * 3 ** -0.5)
                scaled(k["sc1s"][0:S, :], gscs, 1 / 8)
                for i in range(C):
                    ins = dve.tensor_reduce(of[:, i:i + 1], k["ident"][:, V + i:P:C], AX.X, ALU.add)
                link(ins)
                link(scaled(of[:, :], of[:, :], 32 ** -0.5))
                for i in range(C):
                    p = slice(V * i, V * i + V)

                    def component(out, in_):
                        dve.tensor_scalar(out, in_, of[:, i:i + 1], None, ALU.mult)

                    component(k["w0v"][:, i:VC:C], wsc1)
                    component(k["sc1v"][:, i:VC:C], gscv)
                    component(k["w0v"][:, VC + V * i:VC + V * i + V], wl11)
                    component(k["w1v"][:, V * i:V * i + V], gwv)
                    if i < 2:
                        component(k["w1v"][:, V * (i + 3):V * (i + 3) + V], gwv)
                    scaled(k["out0b"][p, 65 + V * i:65 + V * i + V], l2v_b[i], n0)
                    scaled(k["out1b"][p, 96 + V * i:96 + V * i + V], m2v_b[i], n1v)
                    scaled(k["out1c"][p, V * i:V * i + V], m2v_c[i], n1v * 2 ** -0.5)
                dve.drain()


def edges0(nc, t, k, bank, wide):
    ctx, sb, sem = phase(nc)
    with ctx:
        zero = sb("zero1", [P, ZROWS // 2 * AGG1])
        xs = sb("xs", [P, 2, 2, FEAT])
        idx = sb("idx", [P, 2, 2], I32)
        rows = sb("rows", [P, 2, 2], I32)
        e4 = sb("e4", [P, 2, 2, 4])
        e8 = sb("e8", [P, 2, 2, 8])
        ay = sb("ay", [P, 2, 2, 4])
        xT = sb("xT", [P, 2, 2, P])
        eT = sb("eT", [2 * 8, P])
        h1 = sb("h1", [P, P])
        h2 = sb("h2", [P, P])
        w = sb("w", [P, 2, 2, 96])
        dot = sb("dot", [P, 2, C, V])
        dots = sb("dots", [P, 2, V])
        mid = sb("mid", [P, 2, 2, P])
        midT = sb("midT", [P, 2, 2, P])
        yb = sb("yb", [P, 2, 2, FEAT])
        qy = sb("qy", [P, 2, C, V])
        msg = sb("msg", [P, 2, AGG0])
        eq = sb("eq", [P, 2, P])
        total = sb("total", [P, 2, 2, AGG0])
        xTp, hp, wp, midTp, msgp, sump = bank
        xTp4 = xTp[:, :].rearrange("p (j s e) -> p j s e", j=2, s=2)
        midTp4 = midTp[:, :].rearrange("p (j s e) -> p j s e", j=2, s=2)
        wp3 = wp[:, 0:2 * W0N].rearrange("p (j n) -> p j n", j=2)
        msgp3 = msgp[:, 0:2 * MSG0].rearrange("p (j n) -> p j n", j=2)
        sump3 = sump[:, 0:2 * AGG0].rearrange("p (j n) -> p j n", j=2)
        names = ("passed z zd pad idx gx0 gx1 e_in0 e_in1 xTp xT f fw ay wp w01 w23 m1 m3 dot dots midTp midT msgp msgs "
                 "msg eqs sump total0 rows sc00 sc01 sc10 sc11 eTp eT h1p h1 h2p h2 yb ybo0 ybo1 qy").split()
        s = {n: sem("e0_" + n) for n in names}

        def first(q, n):
            return isinstance(q.g, int) and q.g < n

        def last(q):
            return isinstance(q.g, int) and q.g == PAIRS - 1

        def plain(engine):
            engine.sem_inc(s["passed"], 1)

        with nc.Block() as block:

            @block.sync
            def _(sp):
                zt = t["agg1"].rearrange("(p r) c -> p (r c)", p=P)

                def load(q):
                    if not first(q, 2):
                        sp.wait_ge(s["ay"], q.g - 1)
                        sp.wait_ge(s["eTp"], q.g - 1)
                    if last(q):
                        sp.wait_ge(s["pad"], 1)
                    for name, to in (("edge_attr_4", e4), ("edge_attr_8", e8)):
                        if last(q):
                            e = 2 * (PAIRS - 1) * P
                            sp.dma_start(to[:, q.h, 0, :], t[name][e:e + P, :]).then_inc(s[f"e_in{q.h}"], 16)
                            sp.dma_start(to[0:TAIL, q.h, 1, :], t[name][e + P:EDGES, :]).then_inc(s[f"e_in{q.h}"], 16)
                        else:
                            v = t[name][bass.ds(q.g * (2 * P), 2 * P), :].rearrange("(j p) c -> p j c", j=2)
                            sp.dma_start(to[:, q.h, :, :], v).then_inc(s[f"e_in{q.h}"], 16)

                def clear(j, behind):
                    def of(q):
                        n = ZROWS // 2 * AGG1
                        sp.wait_ge(s[behind], q.g + 1)
                        plain(sp)
                        sp.dma_start(zt[:, bass.ds(q.g * (2 * n) + j * n, n)], zero[:, :]).then_inc(s["zd"], 16)
                    return of

                def store(q):
                    sp.wait_ge(s["yb"], q.g + 1)
                    sp.dma_start(t["ybase"][bass.ds(q.g, 1)].rearrange("g p j c -> (g p) j c"), yb[:, q.h, :, :]).then_inc(s[f"ybo{q.h}"], 16)

                sp.wait_ge(s["z"], 1)
                passes(sp, PAIRS, [(-1, clear(0, "rows")), (3, load), (1, store), (0, clear(1, "msgp"))])
                sp.wait_ge(s["zd"], 2 * 16 * NZ)
                sp.wait_ge(s["ybo0"], 16 * (PAIRS // 2))
                sp.wait_ge(s["ybo1"], 16 * (PAIRS // 2))

            @block.gpsimd
            def _(pool):
                pool.memset(zero[:, :], 0.0).then_inc(s["z"], 1)

                def gather(j):
                    def of(q):
                        if j == 0:
                            if not first(q, 2):
                                pool.wait_ge(s[f"gx{q.h}"], q.u * 32)
                                pool.wait_ge(s["yb"], q.g - 1)
                                pool.wait_ge(s["xTp"], q.g - 1)
                            pool.tensor_copy(idx[:, q.h, :], k["src"][:, bass.ds(q.g * 2, 2)]).then_inc(s["idx"], 1)
                            pool.wait_ge(s["idx"], q.g + 1)
                            plain(pool)
                        at = bass.IndirectOffsetOnAxis(ap=idx[:, q.h, j:j + 1], axis=0)
                        pool.indirect_dma_start(xs[:, q.h, j, :], None, t["x"], at).then_inc(s[f"gx{q.h}"], 16)
                    return of

                def pad(q):
                    if last(q):
                        pool.wait_ge(s["ay"], q.g - 1)
                        pool.memset(e4[:, q.h, 1, :], 0.0).then_inc(s["pad"], 1)

                def scatter(j):
                    def of(q):
                        if j == 0:
                            pool.tensor_copy(rows[:, q.h, :], k["row"][:, bass.ds(q.g * 2, 2)]).then_inc(s["rows"], 1)
                            pool.wait_ge(s["rows"], q.g + 1)
                            pool.wait_ge(s["total0"], q.g + 1)
                            if not first(q, 1):
                                pool.wait_ge(s[f"sc{1 - q.h}1"], (q.u + q.h) * 16)
                        else:
                            pool.wait_ge(s[f"sc{q.h}0"], (q.u + 1) * 16)
                        plain(pool)
                        at = bass.IndirectOffsetOnAxis(ap=rows[:, q.h, j:j + 1], axis=0)
                        pool.indirect_dma_start(t["agg0"], at, total[:, q.h, j, :], None,
                                                compute_op=ALU.add).then_inc(s[f"sc{q.h}{j}"], 16)
                    return of

                passes(pool, PAIRS, [(2, pad), (-1, scatter(0)), (3, gather(0)), (-1, scatter(1)), (3, gather(1))])
                for n in ("sc00", "sc01", "sc10", "sc11"):
                    pool.wait_ge(s[n], 16 * (PAIRS // 2))

            @block.tensor
            def _(pe):
                ident = k["ident"]

                def turn(q):
                    pe.wait_ge(s[f"gx{q.h}"], (q.u + 1) * 32)
                    if not first(q, 1):
                        pe.wait_ge(s["xT"], q.g)
                    for j in range(2):
                        pe.transpose(xTp4[:, j, 0, :], xs[:, q.h, j, 0:P], ident[:, :])
                        ins = pe.transpose(xTp4[:, j, 1, :], xs[:, q.h, j, V:FEAT], ident[:, :])
                    ins.then_inc(s["xTp"], 1)

                def turn_edges(q):
                    pe.wait_ge(s[f"e_in{q.h}"], (q.u + 1) * 32 + 32 * last(q))
                    if not first(q, 1):
                        pe.wait_ge(s["h2"], q.g)
                    pe.transpose(hp[0:2 * 8, 2 * P:3 * P], e8[:, q.h, :, :].rearrange("p j c -> p (j c)"),
                                 ident[:, :]).then_inc(s["eTp"], 1)

                def linear(q):
                    pe.wait_ge(s["xT"], q.g + 1)
                    if not first(q, 1):
                        pe.wait_ge(s["fw"], q.g)
                        pe.wait_ge(s["m1"], q.g)
                        pe.wait_ge(s["yb"], q.g)
                    for j in range(2):
                        pe.matmul(wide[:, j, 0:2 * S], xT[:, j, 0, :], k["w0s"][:, :], start=True, stop=True)
                        ins = pe.matmul(wide[:, j, 2 * S:2 * FEAT], xT[:, j, 1, :], k["w0v"][:, :], start=True, stop=True)
                    ins.then_inc(s["f"], 1)

                def network1(q):
                    pe.wait_ge(s["eT"], q.g + 1)
                    pe.matmul(hp[:, 0:P], k["fc1"][:, :], eT[:, :], start=True, stop=True).then_inc(s["h1p"], 1)

                def network2(q):
                    pe.wait_ge(s["h1"], q.g + 1)
                    plain(pe)
                    pe.matmul(hp[:, P:2 * P], k["fc2"][:, :], h1[:, :], start=True, stop=True).then_inc(s["h2p"], 1)

                def network3(q):
                    pe.wait_ge(s["h2"], q.g + 1)
                    if not first(q, 1):
                        pe.wait_ge(s["w01"], q.g)
                        pe.wait_ge(s["w23"], q.g)
                    pe.matmul(wp[:, 0:2 * W0N], h2[:, :], k["fc3"][:, :], start=True, stop=True).then_inc(s["wp"], 1)

                def turn_mid(q):
                    for n in ("m1", "fw", "m3"):
                        pe.wait_ge(s[n], q.g + 1)
                    if not first(q, 1):
                        pe.wait_ge(s["midT"], q.g)
                    for j in range(2):
                        for m in range(2):
                            ins = pe.transpose(midTp4[:, j, m, :], mid[:, j, m, :], ident[:, :])
                    ins.then_inc(s["midTp"], 1)

                def out(q):
                    pe.wait_ge(s["midT"], q.g + 1)
                    if not first(q, 1):
                        pe.wait_ge(s["msgs"], q.g)
                        pe.wait_ge(s["msg"], q.g)
                    for j in range(2):
                        pe.matmul(msgp3[:, j, :], midT[:, j, 0, :], k["out0a"][:, :], start=True, stop=False)
                        ins = pe.matmul(msgp3[:, j, 0:AGG0], midT[:, j, 1, :], k["out0b"][:, :], start=False, stop=True)
                    ins.then_inc(s["msgp"], 1)

                def add_up(q):
                    pe.wait_ge(s["msgs"], q.g + 1)
                    pe.wait_ge(s["msg"], q.g + 1)
                    pe.wait_ge(s["eqs"], q.g + 1)
                    if not first(q, 1):
                        pe.wait_ge(s["total0"], q.g)
                    for j in range(2):
                        ins = pe.matmul(sump3[:, j, :], eq[:, j, :], msg[:, j, :], start=True, stop=True)
                    ins.then_inc(s["sump"], 1)

                passes(pe, PAIRS, [(1, linear), (2, turn_edges), (-1, add_up), (0, turn_mid), (2, network1), (2, turn),
                                   (2, network2), (0, out), (2, network3)])

            @block.scalar
            def _(act):
                def turned(q):
                    act.wait_ge(s["xTp"], q.g + 1)
                    if not first(q, 1):
                        act.wait_ge(s["f"], q.g)
                    act.copy(xT[:, :, :, :], xTp4[:, :, :, :]).then_inc(s["xT"], 1)

                def edges_turned(q):
                    act.wait_ge(s["eTp"], q.g + 1)
                    if not first(q, 1):
                        act.wait_ge(s["h1p"], q.g)
                    act.copy(eT[:, :], hp[0:2 * 8, 2 * P:3 * P]).then_inc(s["eT"], 1)

                def network1(q):
                    act.wait_ge(s["h1p"], q.g + 1)
                    if not first(q, 1):
                        act.wait_ge(s["h2p"], q.g)
                    act.activation(h1[:, :], hp[:, 0:P], ACT.Gelu_apprx_tanh).then_inc(s["h1"], 1)

                def network2(q):
                    act.wait_ge(s["h2p"], q.g + 1)
                    if not first(q, 1):
                        act.wait_ge(s["wp"], q.g)
                    act.activation(h2[:, :], hp[:, P:2 * P], ACT.Gelu_apprx_tanh).then_inc(s["h2"], 1)

                def weights(q):
                    act.wait_ge(s["wp"], q.g + 1)
                    if not first(q, 1):
                        for n in ("m1", "fw", "m3"):
                            act.wait_ge(s[n], q.g)
                    act.copy(w[:, 0, :, :], wp3[:, :, 0:96]).then_inc(s["w01"], 1)

                def mid_turned(q):
                    act.wait_ge(s["midTp"], q.g + 1)
                    if not first(q, 1):
                        act.wait_ge(s["msgp"], q.g)
                    act.copy(midT[:, :, :, :], midTp4[:, :, :, :]).then_inc(s["midT"], 1)

                def scalars_out(q):
                    act.wait_ge(s["msgp"], q.g + 1)
                    if not first(q, 1):
                        act.wait_ge(s["sump"], q.g)
                    act.copy(msg[:, :, 0:S], msgp3[:, :, 0:S])
                    act.copy(msg[:, :, FEAT:AGG0], msgp3[:, :, S:S + 1]).then_inc(s["msgs"], 1)

                def summed(q):
                    act.wait_ge(s["sump"], q.g + 1)
                    if not first(q, 2):
                        act.wait_ge(s[f"sc{q.h}0"], q.u * 16)
                        act.wait_ge(s[f"sc{q.h}1"], q.u * 16)
                    act.copy(total[:, q.h, :, :], sump3[:, :, :]).then_inc(s["total0"], 1)

                def equal(q):
                    if not first(q, 1):
                        act.wait_ge(s["sump"], q.g)
                    act.copy(eq[:, :, :], k["same"][:, bass.ds(q.g * 2, 2), :]).then_inc(s["eqs"], 1)

                passes(act, PAIRS, [(1, weights), (2, edges_turned), (-1, summed), (0, mid_turned), (2, network1),
                                    (2, turned), (2, network2), (0, scalars_out), (0, equal)])

            @block.vector
            def _(dve):
                def attributes(q):
                    dve.wait_ge(s[f"gx{q.h}"], (q.u + 1) * 32)
                    dve.wait_ge(s[f"e_in{q.h}"], (q.u + 1) * 32 + 32 * last(q))
                    if not first(q, 2):
                        dve.wait_ge(s["msg"], q.g - 1)
                    dve.tensor_tensor(ay[:, q.h, :, :], e4[:, q.h, :, :], k["a_src"][:, bass.ds(q.g * 2, 2)].unsqueeze(2).to_broadcast([P, 2, 4]),
                                      ALU.mult).then_inc(s["ay"], 1)

                def product(q):
                    y0 = ay[:, q.h, :, 0:1].to_broadcast([P, 2, 96])
                    y1 = ay[:, q.h, :, 1:4].unsqueeze(3).to_broadcast([P, 2, C, V])
                    fs = wide[:, :, 0:S].unsqueeze(2).to_broadcast([P, 2, 2, S])
                    fv = wide[:, :, 2 * S + VC:2 * FEAT].rearrange("p j (c u) -> p j c u", c=C)
                    dve.wait_ge(s["ay"], q.g + 1)
                    dve.wait_ge(s["f"], q.g + 1)
                    if not first(q, 2):
                        dve.wait_ge(s[f"ybo{q.h}"], q.u * 16)
                    dve.tensor_tensor(dot[:, :, :, :], fv, y1, ALU.mult).then_inc(s["dot"], 1)
                    for j in range(2):
                        ins = dve.scalar_tensor_tensor(yb[:, q.h, j, :], wide[:, j, S:S + FEAT], k["a_src"][:, bass.ds(q.g * 2 + j, 1)],
                                                       xs[:, q.h, j, :], ALU.mult, ALU.add)
                    ins.then_inc(s["yb"], 1)
                    dve.wait_ge(s["dot"], q.g + 1)
                    dve.tensor_reduce(dots[:, :, :], dot[:, :, :, :].rearrange("p j c u -> p j u c"), AX.X,
                                      ALU.add).then_inc(s["dots"], 1)
                    dve.wait_ge(s["w01"], q.g + 1)
                    dve.tensor_tensor(w[:, 1, :, :], wp3[:, :, 96:192], y0, ALU.mult).then_inc(s["w23"], 1)
                    dve.wait_ge(s["w23"], q.g + 1)
                    if not first(q, 1):
                        dve.wait_ge(s["midTp"], q.g)
                    w10 = w[:, :, :, 0:S].rearrange("p m j n -> p j m n")
                    dve.tensor_tensor(mid[:, :, 0, :].rearrange("p j (m n) -> p j m n", m=2), w10, fs, ALU.mult).then_inc(s["m1"], 1)
                    dve.tensor_tensor(mid[:, :, 1, 0:VC].rearrange("p j (c u) -> p j c u", c=C), fv,
                                      w[:, 1, :, 64:96].unsqueeze(2).to_broadcast([P, 2, C, V]), ALU.mult).then_inc(s["fw"], 1)
                    dve.wait_ge(s["dots"], q.g + 1)
                    dve.tensor_tensor(mid[:, :, 1, VC:P], dots[:, :, :], w[:, 0, :, 64:96], ALU.mult).then_inc(s["m3"], 1)

                def vectors_out(q):
                    dve.wait_ge(s["msgs"], q.g + 1)
                    y1 = ay[:, q.h, :, 1:4].unsqueeze(3).to_broadcast([P, 2, C, V])
                    qv = msgp3[:, :, AGG0:MSG0].unsqueeze(2).to_broadcast([P, 2, C, V])
                    dve.tensor_tensor(qy[:, :, :, :], qv, y1, ALU.mult).then_inc(s["qy"], 1)
                    dve.wait_ge(s["qy"], q.g + 1)
                    if not first(q, 1):
                        dve.wait_ge(s["sump"], q.g)
                    dve.tensor_tensor(msg[:, :, S:FEAT].rearrange("p j (u c) -> p j c u", c=C), qy[:, :, :, :],
                                      msgp3[:, :, S + 1:AGG0].rearrange("p j (c u) -> p j c u", c=C),
                                      ALU.add).then_inc(s["msg"], 1)

                passes(dve, PAIRS, [(1, attributes), (1, product), (0, vectors_out)])
                dve.drain()


def edges1(nc, t, k, bank, wide):
    ctx, sb, sem = phase(nc)
    with ctx:
        yb = sb("g_yb", [P, 2, 2, FEAT])
        agg = sb("g_agg", [P, 2, 2, AGG0])
        idx = sb("g_idx", [P, 2, 2], I32)
        rows = sb("g_rows", [P, 2, 2], I32)
        a2 = sb("g_a2", [P, TILES])
        half = sb("g_half", [P, 2])
        e4 = sb("g_e4", [P, 2, 2, 4])
        e64 = sb("g_e64", [P, 2, 2, 64])
        ye = sb("g_ye", [P, 2, 2, 6])
        al = sb("g_al", [P, 2])
        y = sb("g_y", [P, 2, 2, FEAT])
        stats = sb("g_stats", [P, 2, 6])
        mv = sb("g_mv", [P, 2, 2, 2])
        var = sb("g_var", [P, 2])
        rstd = sb("g_rstd", [P, 2])
        ra = sb("g_ra", [P, 2])
        x1 = sb("g_x1", [P, 2, 2, FEAT])
        xT = sb("g_xT", [P, 2, 2, P])
        eT = sb("g_eT", [P, P])
        hid = sb("g_hid", [P, P])
        w = sb("g_w", [P, 2, 2, P])
        dot = sb("g_dot", [P, 2, C, V])
        dots = sb("g_dots", [P, 2, V])
        ca = sb("g_ca", [P, 2, C, V])
        cb = sb("g_cb", [P, 2, C, V])
        cc = sb("g_cc", [P, 2, C, V])
        mid = sb("g_mid", [P, 2, 2, P])
        mid3 = sb("g_mid3", [P, 2, VC])
        midT = sb("g_midT", [P, 2, 2, P])
        mid3T = sb("g_mid3T", [VC, 2, P])
        qy = sb("g_qy", [P, 2, C, V])
        msg = sb("g_msg", [P, 2, AGG1])
        eq = sb("g_eq", [P, 2, P])
        total = sb("g_total", [P, 2, 2, AGG1])
        xTp, hp, wp, midTp, msgp, sump = bank
        xTp4 = xTp[:, :].rearrange("p (j s e) -> p j s e", j=2, s=2)
        midTp4 = midTp[:, :].rearrange("p (j s e) -> p j s e", j=2, s=2)
        wp3 = wp[:, 0:2 * W1N].rearrange("p (j n) -> p j n", j=2)
        HW = S + 5 * V
        hvp = wide[:, 0, 0:2 * HW].rearrange("p (j n) -> p j n", j=2)
        mid3Tp = wide[:, 1, 0:2 * P].rearrange("p (j e) -> p j e", j=2)
        msgp3 = msgp[:, 0:2 * MSG1].rearrange("p (j n) -> p j n", j=2)
        sump3 = sump[:, 0:2 * AGG1].rearrange("p (j n) -> p j n", j=2)
        names = ("passed half a2 idx in0 in1 yin0 yin1 ein0 ein1 pad al y st mv var rstd ra x1 ye xTp eTp xT eT f h1p h1 wp wa wb m0 m1 "
                 "dot dots m2 ca cc m3 midTp mid3Tp midT mid3T msgp msgs msg qy eqs sump total0 rows sc00 sc01 sc10 sc11").split()
        s = {n: sem("e1_" + n) for n in names}

        def first(q, n):
            return isinstance(q.g, int) and q.g < n

        def last(q):
            return isinstance(q.g, int) and q.g == PAIRS - 1

        def plain(engine):
            engine.sem_inc(s["passed"], 1)

        with nc.Block() as block:

            @block.sync
            def _(sp):
                def load(q):
                    if not first(q, 2):
                        sp.wait_ge(s["y"], q.g - 1)
                    sp.dma_start(yb[:, q.h, :, :], t["ybase"][bass.ds(q.g, 1)].rearrange("g p j c -> (g p) j c")).then_inc(s[f"yin{q.h}"], 16)

                def load_edges(q):
                    if not first(q, 2):
                        sp.wait_ge(s["ye"], q.g - 1)
                        sp.wait_ge(s["eTp"], q.g - 1)
                    if last(q):
                        sp.wait_ge(s["pad"], 1)
                    for name, to in (("edge_attr_4", e4), ("edge_attr_64", e64)):
                        if last(q):
                            e = 2 * (PAIRS - 1) * P
                            sp.dma_start(to[:, q.h, 0, :], t[name][e:e + P, :]).then_inc(s[f"ein{q.h}"], 16)
                            sp.dma_start(to[0:TAIL, q.h, 1, :], t[name][e + P:EDGES, :]).then_inc(s[f"ein{q.h}"], 16)
                        else:
                            v = t[name][bass.ds(q.g * (2 * P), 2 * P), :].rearrange("(j p) c -> p j c", j=2)
                            sp.dma_start(to[:, q.h, :, :], v).then_inc(s[f"ein{q.h}"], 16)

                passes(sp, PAIRS, [(4, load), (3, load_edges)])

            @block.gpsimd
            def _(pool):
                pool.memset(half[:, :], -0.5).then_inc(s["half"], 1)
                pool.wait_ge(s["half"], 1)

                def gather(j):
                    def of(q):
                        if j == 0:
                            if not first(q, 2):
                                pool.wait_ge(s[f"in{q.h}"], q.u * 32)
                                pool.wait_ge(s["y"], q.g - 1)
                            pool.tensor_copy(idx[:, q.h, :], k["src"][:, bass.ds(q.g * 2, 2)]).then_inc(s["idx"], 1)
                            pool.wait_ge(s["idx"], q.g + 1)
                            plain(pool)
                        at = bass.IndirectOffsetOnAxis(ap=idx[:, q.h, j:j + 1], axis=0)
                        pool.indirect_dma_start(agg[:, q.h, j, :], None, t["agg0"], at).then_inc(s[f"in{q.h}"], 16)
                    return of

                def pad(q):
                    if last(q):
                        pool.wait_ge(s["ye"], q.g - 1)
                        pool.memset(e4[:, q.h, 1, :], 0.0).then_inc(s["pad"], 1)

                def root(q):
                    pool.wait_ge(s["var"], q.g + 1)
                    if not first(q, 1):
                        pool.wait_ge(s["ra"], q.g)
                    pool.tensor_tensor(rstd[:, :], var[:, :], half[:, :], ALU.pow).then_inc(s["rstd"], 1)

                def scatter(j):
                    def of(q):
                        if j == 0:
                            pool.tensor_copy(rows[:, q.h, :], k["row"][:, bass.ds(q.g * 2, 2)]).then_inc(s["rows"], 1)
                            pool.wait_ge(s["rows"], q.g + 1)
                            pool.wait_ge(s["total0"], q.g + 1)
                            if not first(q, 1):
                                pool.wait_ge(s[f"sc{1 - q.h}1"], (q.u + q.h) * 16)
                        else:
                            pool.wait_ge(s[f"sc{q.h}0"], (q.u + 1) * 16)
                        plain(pool)
                        at = bass.IndirectOffsetOnAxis(ap=rows[:, q.h, j:j + 1], axis=0)
                        pool.indirect_dma_start(t["agg1"], at, total[:, q.h, j, :], None,
                                                compute_op=ALU.add).then_inc(s[f"sc{q.h}{j}"], 16)
                    return of

                passes(pool, PAIRS, [(2, pad), (-1, scatter(0)), (4, gather(0)), (-1, scatter(1)), (4, gather(1)), (3, root)])
                for n in ("sc00", "sc01", "sc10", "sc11"):
                    pool.wait_ge(s[n], 16 * (PAIRS // 2))

            @block.tensor
            def _(pe):
                ident = k["ident"]

                def turn(q):
                    pe.wait_ge(s["x1"], q.g + 1)
                    if not first(q, 1):
                        pe.wait_ge(s["xT"], q.g)
                    for j in range(2):
                        pe.transpose(xTp4[:, j, 0, :], x1[:, q.h, j, 0:P], ident[:, :])
                        ins = pe.transpose(xTp4[:, j, 1, :], x1[:, q.h, j, V:FEAT], ident[:, :])
                    ins.then_inc(s["xTp"], 1)

                def turn_edges(q):
                    pe.wait_ge(s[f"ein{q.h}"], (q.u + 1) * 32 + 32 * last(q))
                    if not first(q, 1):
                        pe.wait_ge(s["h1"], q.g)
                    plain(pe)
                    pe.transpose(hp[:, 0:P], e64[:, q.h, :, :].rearrange("p j c -> p (j c)"),
                                 ident[:, :]).then_inc(s["eTp"], 1)

                def linear(q):
                    pe.wait_ge(s["xT"], q.g + 1)
                    if not first(q, 1):
                        pe.wait_ge(s["m1"], q.g)
                    for j in range(2):
                        pe.matmul(hvp[:, j, 0:S], xT[:, j, 0, :], k["w1s"][:, :], start=True, stop=True)
                        ins = pe.matmul(hvp[:, j, S:HW], xT[:, j, 1, :], k["w1v"][:, :], start=True, stop=True)
                    ins.then_inc(s["f"], 1)

                def network1(q):
                    pe.wait_ge(s["eT"], q.g + 1)
                    plain(pe)
                    pe.matmul(hp[:, P:2 * P], k["gfc1"][:, :], eT[:, :], start=True, stop=True).then_inc(s["h1p"], 1)

                def network2(q):
                    pe.wait_ge(s["h1"], q.g + 1)
                    if not first(q, 1):
                        pe.wait_ge(s["wb"], q.g)
                    pe.matmul(wp[:, 0:2 * W1N], hid[:, :], k["gfc2"][:, :], start=True, stop=True).then_inc(s["wp"], 1)

                def turn_mid(q):
                    pe.wait_ge(s["m1"], q.g + 1)
                    pe.wait_ge(s["m2"], q.g + 1)
                    if not first(q, 1):
                        pe.wait_ge(s["midT"], q.g)
                    for j in range(2):
                        for m in range(2):
                            ins = pe.transpose(midTp4[:, j, m, :], mid[:, j, m, :], ident[:, :])
                    ins.then_inc(s["midTp"], 1)
                    pe.wait_ge(s["m3"], q.g + 1)
                    if not first(q, 1):
                        pe.wait_ge(s["mid3T"], q.g)
                    for j in range(2):
                        ins = pe.transpose(mid3Tp[0:VC, j, :], mid3[:, j, :], ident[:, :])
                    ins.then_inc(s["mid3Tp"], 1)

                def out(q):
                    pe.wait_ge(s["midT"], q.g + 1)
                    pe.wait_ge(s["mid3T"], q.g + 1)
                    if not first(q, 1):
                        pe.wait_ge(s["msg"], q.g)
                    for j in range(2):
                        pe.matmul(msgp3[:, j, :], midT[:, j, 0, :], k["out1a"][:, :], start=True, stop=False)
                        pe.matmul(msgp3[:, j, 0:AGG1], midT[:, j, 1, :], k["out1b"][:, :], start=False, stop=False)
                        ins = pe.matmul(msgp3[:, j, 96:AGG1], mid3T[:, j, :], k["out1c"][:, :], start=False, stop=True)
                    ins.then_inc(s["msgp"], 1)

                def add_up(q):
                    pe.wait_ge(s["msg"], q.g + 1)
                    pe.wait_ge(s["eqs"], q.g + 1)
                    if not first(q, 1):
                        pe.wait_ge(s["total0"], q.g)
                    for j in range(2):
                        ins = pe.matmul(sump3[:, j, :], eq[:, j, :], msg[:, j, :], start=True, stop=True)
                    ins.then_inc(s["sump"], 1)

                passes(pe, PAIRS, [(1, linear), (2, turn_edges), (-1, add_up), (0, turn_mid), (2, network1),
                                   (0, out), (2, turn), (2, network2)])

            @block.scalar
            def _(act):
                def turned(q):
                    act.wait_ge(s["xTp"], q.g + 1)
                    if not first(q, 1):
                        act.wait_ge(s["f"], q.g)
                    act.copy(xT[:, :, :, :], xTp4[:, :, :, :]).then_inc(s["xT"], 1)

                def edges_turned(q):
                    act.wait_ge(s["eTp"], q.g + 1)
                    if not first(q, 1):
                        act.wait_ge(s["h1p"], q.g)
                    act.copy(eT[:, :], hp[:, 0:P]).then_inc(s["eT"], 1)

                def network(q):
                    act.wait_ge(s["h1p"], q.g + 1)
                    if not first(q, 1):
                        act.wait_ge(s["wp"], q.g)
                    act.activation(hid[:, :], hp[:, P:2 * P], ACT.Silu).then_inc(s["h1"], 1)

                def weights(q):
                    act.wait_ge(s["wp"], q.g + 1)
                    if not first(q, 1):
                        for n in ("m0", "m2", "m3"):
                            act.wait_ge(s[n], q.g)
                    act.copy(w[:, 0, :, :], wp3[:, :, 0:P]).then_inc(s["wa"], 1)

                def mid_turned(q):
                    act.wait_ge(s["midTp"], q.g + 1)
                    if not first(q, 1):
                        act.wait_ge(s["msgp"], q.g)
                    act.copy(midT[:, :, :, :], midTp4[:, :, :, :]).then_inc(s["midT"], 1)
                    act.wait_ge(s["mid3Tp"], q.g + 1)
                    act.copy(mid3T[:, :, :], mid3Tp[0:VC, :, :]).then_inc(s["mid3T"], 1)

                def scalars_out(q):
                    act.wait_ge(s["msgp"], q.g + 1)
                    if not first(q, 1):
                        act.wait_ge(s["sump"], q.g)
                    act.copy(msg[:, :, 0:96], msgp3[:, :, 0:96]).then_inc(s["msgs"], 1)

                def summed(q):
                    act.wait_ge(s["sump"], q.g + 1)
                    if not first(q, 2):
                        act.wait_ge(s[f"sc{q.h}0"], q.u * 16)
                        act.wait_ge(s[f"sc{q.h}1"], q.u * 16)
                    act.copy(total[:, q.h, :, :], sump3[:, :, :]).then_inc(s["total0"], 1)

                def equal(q):
                    if not first(q, 1):
                        act.wait_ge(s["sump"], q.g)
                    act.copy(eq[:, :, :], k["same"][:, bass.ds(q.g * 2, 2), :]).then_inc(s["eqs"], 1)

                passes(act, PAIRS, [(1, weights), (2, edges_turned), (-1, summed), (0, mid_turned), (2, network),
                                    (0, scalars_out), (2, turned), (0, equal)])

            @block.vector
            def _(dve):
                dve.tensor_tensor(a2[:, :], k["a_src"][:, :], k["a_src"][:, :], ALU.mult).then_inc(s["a2"], 1)
                dve.wait_ge(s["a2"], 1)

                def layer0(q):
                    dve.wait_ge(s[f"in{q.h}"], (q.u + 1) * 32)
                    dve.wait_ge(s[f"yin{q.h}"], (q.u + 1) * 16)
                    dve.tensor_tensor(al[:, :], agg[:, q.h, :, FEAT], a2[:, bass.ds(q.g * 2, 2)], ALU.mult).then_inc(s["al"], 1)
                    dve.wait_ge(s["al"], q.g + 1)
                    for j in range(2):
                        ins = dve.scalar_tensor_tensor(y[:, q.h, j, :], agg[:, q.h, j, 0:FEAT], al[:, j:j + 1],
                                                       yb[:, q.h, j, :], ALU.mult, ALU.add)
                    ins.then_inc(s["y"], 1)
                    dve.wait_ge(s["y"], q.g + 1)
                    for j in range(2):
                        ins = dve.bn_stats(stats[:, j, :], y[:, q.h, j, :])
                    ins.then_inc(s["st"], 1)
                    dve.wait_ge(s["st"], q.g + 1)
                    plain(dve)
                    for j in range(2):
                        ins = dve.bn_aggr(mv[:, q.h, j, :], stats[:, j, :])
                    ins.then_inc(s["mv"], 1)
                    dve.wait_ge(s["mv"], q.g + 1)
                    if not first(q, 1):
                        dve.wait_ge(s["rstd"], q.g)
                    dve.tensor_scalar(var[:, :], mv[:, q.h, :, 1], EPS, None, ALU.add).then_inc(s["var"], 1)

                def norm(q):
                    dve.wait_ge(s["rstd"], q.g + 1)
                    dve.tensor_tensor(ra[:, :], rstd[:, :], k["a_src"][:, bass.ds(q.g * 2, 2)], ALU.mult).then_inc(s["ra"], 1)
                    dve.wait_ge(s["ra"], q.g + 1)
                    if not first(q, 2):
                        dve.wait_ge(s["xTp"], q.g - 1)
                    for j in range(2):
                        ins = dve.tensor_scalar(x1[:, q.h, j, :], y[:, q.h, j, :], mv[:, q.h, j, 0:1], ra[:, j:j + 1],
                                                ALU.subtract, ALU.mult)
                    ins.then_inc(s["x1"], 1)

                def attributes(q):
                    dve.wait_ge(s[f"ein{q.h}"], (q.u + 1) * 32 + 32 * last(q))
                    dve.tensor_copy(ye[:, q.h, :, 0:3], e4[:, q.h, :, 1:4])
                    dve.tensor_copy(ye[:, q.h, :, 3:5], e4[:, q.h, :, 1:3])
                    dve.tensor_copy(ye[:, q.h, :, 5:6], e4[:, q.h, :, 0:1]).then_inc(s["ye"], 1)

                def product(q):
                    hs = hvp[:, :, 0:S].unsqueeze(2).to_broadcast([P, 2, 2, S])
                    hv = hvp[:, :, S:HW].rearrange("p j (c u) -> p j c u", c=5)
                    yc = [ye[:, q.h, :, c:c + 3].unsqueeze(3).to_broadcast([P, 2, C, V]) for c in range(3)]
                    y0 = ye[:, q.h, :, 5:6].to_broadcast([P, 2, 96])
                    dve.wait_ge(s["ye"], q.g + 1)
                    dve.wait_ge(s["f"], q.g + 1)
                    dve.tensor_tensor(ca[:, :, :, :], hv[:, :, 1:4, :], yc[2], ALU.mult)
                    dve.tensor_tensor(cb[:, :, :, :], hv[:, :, 2:5, :], yc[1], ALU.mult).then_inc(s["ca"], 1)
                    dve.tensor_tensor(dot[:, :, :, :], hv[:, :, 0:3, :], yc[0], ALU.mult).then_inc(s["dot"], 1)
                    dve.wait_ge(s["ca"], q.g + 1)
                    dve.tensor_tensor(cc[:, :, :, :], ca[:, :, :, :], cb[:, :, :, :], ALU.subtract).then_inc(s["cc"], 1)
                    dve.wait_ge(s["dot"], q.g + 1)
                    dve.tensor_reduce(dots[:, :, :], dot[:, :, :, :].rearrange("p j c u -> p j u c"), AX.X,
                                      ALU.add).then_inc(s["dots"], 1)
                    dve.wait_ge(s["wa"], q.g + 1)
                    dve.tensor_tensor(w[:, 1, :, 0:96], wp3[:, :, P:W1N], y0, ALU.mult).then_inc(s["wb"], 1)
                    dve.wait_ge(s["cc"], q.g + 1)
                    if not first(q, 1):
                        dve.wait_ge(s["midTp"], q.g)
                        dve.wait_ge(s["mid3Tp"], q.g)
                    dve.tensor_tensor(mid3[:, :, :].rearrange("p j (c u) -> p j c u", c=C), cc[:, :, :, :],
                                      w[:, 0, :, 96:P].unsqueeze(2).to_broadcast([P, 2, C, V]), ALU.mult).then_inc(s["m3"], 1)
                    dve.wait_ge(s["dots"], q.g + 1)
                    dve.tensor_tensor(mid[:, :, 1, VC:P], dots[:, :, :], w[:, 0, :, 64:96], ALU.mult).then_inc(s["m2"], 1)
                    dve.wait_ge(s["wb"], q.g + 1)
                    dve.tensor_tensor(mid[:, :, 0, :].rearrange("p j (m n) -> p j m n", m=2),
                                      w[:, :, :, 0:S].rearrange("p m j n -> p j m n"), hs, ALU.mult).then_inc(s["m0"], 1)
                    dve.tensor_tensor(mid[:, :, 1, 0:VC].rearrange("p j (c u) -> p j c u", c=C), hv[:, :, 0:3, :],
                                      w[:, 1, :, 64:96].unsqueeze(2).to_broadcast([P, 2, C, V]), ALU.mult).then_inc(s["m1"], 1)

                def vectors_out(q):
                    dve.wait_ge(s["msgs"], q.g + 1)
                    y1 = ye[:, q.h, :, 0:3].unsqueeze(3).to_broadcast([P, 2, C, V])
                    qv = msgp3[:, :, AGG1:MSG1].unsqueeze(2).to_broadcast([P, 2, C, V])
                    dve.tensor_tensor(qy[:, :, :, :], qv, y1, ALU.mult).then_inc(s["qy"], 1)
                    dve.wait_ge(s["qy"], q.g + 1)
                    if not first(q, 1):
                        dve.wait_ge(s["sump"], q.g)
                    dve.tensor_tensor(msg[:, :, 96:AGG1].rearrange("p j (u c) -> p j c u", c=C), qy[:, :, :, :],
                                      msgp3[:, :, 96:AGG1].rearrange("p j (c u) -> p j c u", c=C),
                                      ALU.add).then_inc(s["msg"], 1)

                passes(dve, PAIRS, [(1, attributes), (1, product), (2, norm), (3, layer0), (0, vectors_out)])
                dve.drain()


def nodes(nc, t, k, bank, wide, other):
    ctx, sb, sem = phase(nc)
    with ctx:
        x = sb("n_x", [P, 2, J, FEAT])
        s0 = sb("n_s0", [P, 2, J, AGG0])
        s1 = sb("n_s1", [P, 2, J, AGG1])
        a = sb("n_a", [P, NGROUPS, J])
        a2 = sb("n_a2", [P, NGROUPS, J])
        half = sb("n_half", [P, J])
        xsT = sb("n_xsT", [P, J * P])
        xvT = sb("n_xvT", [P, J * P])
        al = sb("n_al", [P, J])
        b = sb("n_b", [P, 2, J, FEAT])
        y = sb("n_y", [P, 2, J, FEAT])
        stats = sb("n_stats", [P, J, 6])
        mv = sb("n_mv", [P, 2, J, 2])
        var = sb("n_var", [P, J])
        rstd = sb("n_rstd", [P, 2, J])
        shift = sb("n_shift", [P, 2, J])
        x1 = sb("n_x1", [P, 2, J, FEAT])
        x1sT = sb("n_x1sT", [P, J * P])
        x1vT = sb("n_x1vT", [P, J * P])
        gate = sb("n_gate", [P, J, 96])
        m = sb("n_m", [P, J, FEAT])
        z = sb("n_z", [P, 2, J, FEAT])
        stats1 = sb("n_stats1", [P, J, 6])
        mv1 = sb("n_mv1", [P, 2, J, 2])
        var1 = sb("n_var1", [P, J])
        rstd1 = sb("n_rstd1", [P, 2, J])
        shift1 = sb("n_shift1", [P, 2, J])
        res = sb("n_res", [P, 2, J, FEAT])
        names = ("passed half a in0 in1 s1in0 s1in1 xT xTc sc a2 al b0 b y st mv var rstd shift x1 x1T x1Tc pre gate ms m z "
                 "st1 mv1 var1 rstd1 shift1 ra rp out0 out1").split()
        s = {n: sem("n_" + n) for n in names}
        scp = wide[:, :, 0:2 * FEAT].rearrange("p b (i c) -> p b i c", i=2)
        prep = other[:, :, 0:2 * AGG1].rearrange("p b (i c) -> p b i c", i=2)

        def first(q, n):
            return isinstance(q.g, int) and q.g < n

        def last(q):
            return isinstance(q.g, int) and q.g == NGROUPS - 1

        def part(name, q):
            v = t[name][NODES - J * P:NODES, :] if last(q) else t[name][bass.ds(q.g * (J * P), J * P), :]
            return v.rearrange("(p j) c -> p (j c)", j=J)

        def rows(v):
            return v.rearrange("p j c -> p (j c)")

        def four(v):
            return v.rearrange("p (b i) c -> p b i c", b=2)

        def a1(q, j):
            return a[:, bass.ds(q.g, 1), j:j + 1].rearrange("p g j -> p (g j)")

        def plain(engine):
            engine.sem_inc(s["passed"], 1)

        with nc.Block() as block:

            @block.sync
            def _(sp):
                whole = (NGROUPS - 1) * J * P
                sp.dma_start(a[:, 0:NGROUPS - 1, :],
                             t["node_vec1"][0:whole, :].rearrange("(g p j) c -> p g (j c)", p=P, j=J)).then_inc(s["a"], 16)
                sp.dma_start(a[:, NGROUPS - 1, :],
                             t["node_vec1"][NODES - J * P:NODES, :].rearrange("(p j) c -> p (j c)", j=J)).then_inc(s["a"], 16)

                def load(q):
                    if not first(q, 2):
                        sp.wait_ge(s["xT"], q.g - 1)
                        sp.wait_ge(s["b"], q.g - 1)
                    sp.dma_start(rows(x[:, q.h, :, :]), part("x", q)).then_inc(s[f"in{q.h}"], 16)
                    sp.dma_start(rows(s0[:, q.h, :, :]), part("agg0", q)).then_inc(s[f"in{q.h}"], 16)

                def load1(q):
                    if not first(q, 2):
                        sp.wait_ge(s["pre"], q.g - 1)
                    sp.dma_start(rows(s1[:, q.h, :, :]), part("agg1", q)).then_inc(s[f"s1in{q.h}"], 16)

                def store(q):
                    sp.wait_ge(s["ra"], q.g + 1)
                    sp.wait_ge(s["rp"], q.g + 1)
                    if last(q):
                        sp.wait_ge(s[f"out{1 - q.h}"], (q.u + q.h) * 16)
                    sp.dma_start(part("out", q), rows(res[:, q.h, :, :])).then_inc(s[f"out{q.h}"], 16)

                passes(sp, NGROUPS, [(6, load), (2, load1), (-1, store)])
                for n in ("out0", "out1"):
                    sp.wait_ge(s[n], 16 * (NGROUPS // 2))

            @block.gpsimd
            def _(pool):
                pool.memset(half[:, :], -0.5).then_inc(s["half"], 1)
                pool.wait_ge(s["half"], 1)
                pool.wait_ge(s["a"], 32)
                pool.tensor_tensor(a2[:, :, :], a[:, :, :], a[:, :, :], ALU.mult).then_inc(s["a2"], 1)
                pool.wait_ge(s["a2"], 1)

                def root(v, r, vs, rs, free):
                    def of(q):
                        pool.wait_ge(s[vs], q.g + 1)
                        if not first(q, 2):
                            pool.wait_ge(s[free], q.g - 1)
                        pool.tensor_tensor(r[:, q.h, :], v[:, :], half[:, :], ALU.pow).then_inc(s[rs], 1)
                    return of

                def sums0(q):
                    pool.wait_ge(s[f"in{q.h}"], (q.u + 1) * 32)
                    plain(pool)
                    pool.tensor_tensor(al[:, :], s0[:, q.h, :, FEAT],
                                       a2[:, bass.ds(q.g, 1), :].rearrange("p g j -> p (g j)"), ALU.mult).then_inc(s["al"], 1)
                    pool.wait_ge(s["al"], q.g + 1)
                    if not first(q, 2):
                        pool.wait_ge(s["y"], q.g - 1)
                    pool.tensor_tensor(b[:, q.h, :, :], s0[:, q.h, :, 0:FEAT],
                                       al[:, :].unsqueeze(2).to_broadcast([P, J, FEAT]), ALU.mult).then_inc(s["b0"], 1)
                    pool.wait_ge(s["b0"], q.g + 1)
                    pool.tensor_tensor(b[:, q.h, :, :], b[:, q.h, :, :], x[:, q.h, :, :], ALU.add).then_inc(s["b"], 1)

                def norm1(q):
                    pool.wait_ge(s["shift1"], q.g + 1)
                    if not first(q, 2):
                        pool.wait_ge(s[f"out{q.h}"], q.u * 16)
                    plain(pool)
                    for j in range(NACT, J):
                        ins = pool.tensor_scalar(res[:, q.h, j, :], z[:, q.h, j, :], rstd1[:, q.h, j:j + 1],
                                                 shift1[:, q.h, j:j + 1], ALU.mult, ALU.add)
                    ins.then_inc(s["rp"], 1)

                passes(pool, NGROUPS, [(-1, root(var1, rstd1, "var1", "rstd1", "ra")),
                                       (2, root(var, rstd, "var", "rstd", "x1")), (5, sums0), (-1, norm1)])

            @block.tensor
            def _(pe):
                ident = k["ident"]

                def product1(q):
                    pe.wait_ge(s["x1Tc"], q.g + 1)
                    pe.wait_ge(s[f"s1in{q.h}"], (q.u + 1) * 16)
                    if not first(q, 1):
                        pe.wait_ge(s["m"], q.g)
                    for j in range(J):
                        o = prep[:, j // 2, j % 2, :]
                        pe.matmul(o, ident[:, :], s1[:, q.h, j, :], start=True, stop=False)
                        pe.matmul(o[:, 0:96], x1sT[:, j * P:j * P + P], k["sc1s"][:, :], start=False, stop=False)
                        ins = pe.matmul(o[:, 96:AGG1], x1vT[:, j * P:j * P + P], k["sc1v"][:, :], start=False, stop=True)
                    ins.then_inc(s["pre"], 1)

                def turn(src, banks, ready, free, done):
                    def of(q):
                        pe.wait_ge(*ready(q))
                        if not first(q, 1):
                            pe.wait_ge(s[free], q.g)
                        plain(pe)
                        for j in range(J):
                            pe.transpose(banks[0][:, j * P:j * P + P], src[:, q.h, j, 0:P], ident[:, :])
                            ins = pe.transpose(banks[1][:, j * P:j * P + P], src[:, q.h, j, V:FEAT], ident[:, :])
                        ins.then_inc(s[done], 1)
                    return of

                def product0(q):
                    pe.wait_ge(s["xTc"], q.g + 1)
                    if not first(q, 1):
                        pe.wait_ge(s["y"], q.g)
                    for j in range(J):
                        o = scp[:, j // 2, j % 2, :]
                        pe.matmul(o[:, 0:S], xsT[:, j * P:j * P + P], k["w0s"][:, S:2 * S], start=True, stop=True)
                        ins = pe.matmul(o[:, S:FEAT], xvT[:, j * P:j * P + P], k["w0v"][:, 0:VC], start=True, stop=True)
                    ins.then_inc(s["sc"], 1)

                passes(pe, NGROUPS, [
                    (1, turn(x1, bank[2:4], lambda q: (s["x1"], q.g + 1), "x1Tc", "x1T")),
                    (4, product0),
                    (5, turn(x, bank[0:2], lambda q: (s[f"in{q.h}"], (q.u + 1) * 32), "xTc", "xT")),
                    (1, product1)])

            @block.scalar
            def _(act):
                act.wait_ge(s["a"], 32)

                def gates(q):
                    act.wait_ge(s["pre"], q.g + 1)
                    if not first(q, 1):
                        act.wait_ge(s["m"], q.g)
                    for j in range(J):
                        ins = act.activation(gate[:, j, :], prep[:, j // 2, j % 2, 0:96], ACT.Sigmoid, scale=a1(q, j))
                    ins.then_inc(s["gate"], 1)

                def turned(banks, to, ready, free, done):
                    def of(q):
                        act.wait_ge(s[ready], q.g + 1)
                        if not first(q, 1):
                            act.wait_ge(s[free], q.g)
                        act.copy(to[0][:, :], banks[0][:, :])
                        act.copy(to[1][:, :], banks[1][:, :]).then_inc(s[done], 1)
                    return of

                def norm0(q):
                    act.wait_ge(s["shift"], q.g + 1)
                    if not first(q, 2):
                        act.wait_ge(s["z"], q.g - 1)
                        act.wait_ge(s["x1T"], q.g - 1)
                    for j in range(J):
                        ins = act.activation(x1[:, q.h, j, :], y[:, q.h, j, :], ACT.Identity, bias=shift[:, q.h, j:j + 1],
                                             scale=rstd[:, q.h, j:j + 1])
                    ins.then_inc(s["x1"], 1)

                def norm1(q):
                    act.wait_ge(s["shift1"], q.g + 1)
                    if not first(q, 2):
                        act.wait_ge(s[f"out{q.h}"], q.u * 16)
                    for j in range(NACT):
                        ins = act.activation(res[:, q.h, j, :], z[:, q.h, j, :], ACT.Identity,
                                             bias=shift1[:, q.h, j:j + 1], scale=rstd1[:, q.h, j:j + 1])
                    ins.then_inc(s["ra"], 1)

                passes(act, NGROUPS, [(1, turned(bank[2:4], (x1sT, x1vT), "x1T", "pre", "x1Tc")), (-1, norm1), (2, norm0),
                                      (5, turned(bank[0:2], (xsT, xvT), "xT", "sc", "xTc")), (1, gates)])

            @block.vector
            def _(dve):
                dve.wait_ge(s["a"], 32)

                def moments(y_, st, ready, n):
                    def of(q):
                        dve.wait_ge(s[ready], q.g + 1)
                        for j in range(J):
                            ins = dve.bn_stats(st[:, j, :], y_[:, q.h, j, :])
                        ins.then_inc(s["st" + n], 1)
                    return of

                def joined(st, mv_, n):
                    def of(q):
                        dve.wait_ge(s["st" + n], q.g + 1)
                        plain(dve)
                        for j in range(J):
                            ins = dve.bn_aggr(mv_[:, q.h, j, :], st[:, j, :])
                        ins.then_inc(s["mv" + n], 1)
                    return of

                def guarded(mv_, v, n):
                    def of(q):
                        dve.wait_ge(s["mv" + n], q.g + 1)
                        if not first(q, 1):
                            dve.wait_ge(s["rstd" + n], q.g)
                        dve.tensor_scalar(v[:, :], mv_[:, q.h, :, 1], EPS, None, ALU.add).then_inc(s["var" + n], 1)
                    return of

                def layer0(q):
                    dve.wait_ge(s["sc"], q.g + 1)
                    dve.wait_ge(s["b"], q.g + 1)
                    if not first(q, 2):
                        dve.wait_ge(s["x1"], q.g - 1)
                    for j in range(J):
                        ins = dve.scalar_tensor_tensor(y[:, q.h, j, :], scp[:, j // 2, j % 2, :], a1(q, j), b[:, q.h, j, :],
                                                       ALU.mult, ALU.add)
                    ins.then_inc(s["y"], 1)

                def gated(q):
                    dve.wait_ge(s["gate"], q.g + 1)
                    dve.tensor_tensor(four(m[:, :, 0:S]), prep[:, :, :, 0:S], four(gate[:, :, 0:S]), ALU.mult).then_inc(s["ms"], 1)
                    for d in range(2):
                        ins = dve.tensor_tensor(
                            m[:, 2 * d:2 * d + 2, S:FEAT].rearrange("p j (u c) -> p j u c", c=C),
                            prep[:, d, :, 96:AGG1].rearrange("p j (u c) -> p j u c", c=C),
                            gate[:, 2 * d:2 * d + 2, S:96].unsqueeze(3).to_broadcast([P, 2, V, C]), ALU.mult)
                    ins.then_inc(s["m"], 1)

                def layer1(q):
                    dve.wait_ge(s["m"], q.g + 1)
                    if not first(q, 2):
                        dve.wait_ge(s["ra"], q.g - 1)
                        dve.wait_ge(s["rp"], q.g - 1)
                    for j in range(J):
                        ins = dve.scalar_tensor_tensor(z[:, q.h, j, :], m[:, j, :], a1(q, j), x1[:, q.h, j, :],
                                                       ALU.mult, ALU.add)
                    ins.then_inc(s["z"], 1)

                def shifts(mv_, r, to, rs, done):
                    def of(q):
                        dve.wait_ge(s[rs], q.g + 1)
                        dve.scalar_tensor_tensor(to[:, q.h, :], mv_[:, q.h, :, 0], -1.0, r[:, q.h, :], ALU.mult,
                                                 ALU.mult).then_inc(s[done], 1)
                    return of

                passes(dve, NGROUPS, [
                    (3, layer0),
                    (3, moments(y, stats, "y", "")),
                    (0, gated),
                    (-1, shifts(mv1, rstd1, shift1, "rstd1", "shift1")),
                    (2, shifts(mv, rstd, shift, "rstd", "shift")),
                    (0, layer1),
                    (3, joined(stats, mv, "")),
                    (0, moments(z, stats1, "z", "1")),
                    (3, guarded(mv, var, "")),
                    (0, joined(stats1, mv1, "1")),
                    (0, guarded(mv1, var1, "1"))])
                dve.drain()


SCRATCH = {"agg0": (TABLE, AGG0), "agg1": (TABLE, AGG1), "ybase": (PAIRS, P, 2, FEAT)}


def kernel(**inputs):
    import numpy as _np
    import concourse.bacc as _bacc
    from concourse.bass_utils import run_bass_kernel_spmd as _run

    nc = _bacc.Bacc("TRN2", target_bir_lowering=False, num_devices=1)
    arrays, t = {}, {}
    for name, given in inputs.items():
        a = _np.ascontiguousarray(given)
        arrays[f"in_{name}"] = a
        t[name] = nc.dram_tensor(f"in_{name}", a.shape, mybir.dt.from_np(a.dtype), kind="ExternalInput").ap()
    for name, shape in SCRATCH.items():
        t[name] = nc.dram_tensor(f"d_{name}", list(shape), F32, kind="Internal").ap()
    t["out"] = nc.dram_tensor("out", [NODES, FEAT], F32, kind="ExternalOutput").ap()
    build(nc, t)
    r = _run(nc, [arrays], core_ids=[0])
    return r.results[0]["out"]
```
